# Optimizing a Trainium2 kernel written in Bass

```python
import numpy as np
import jax
import jax.numpy as jnp

def _softmax(x, axis=-1):
    return jax.nn.softmax(x, axis=axis)

def _gelu(x):
    return jax.nn.gelu(x, approximate=True)

def _silu(x):
    return jax.nn.silu(x)

def _sigmoid(x):
    return jax.nn.sigmoid(x)

def _layernorm(x, axis=-1, eps=1e-05):
    m = jnp.mean(x, axis=axis, keepdims=True)
    v = jnp.var(x, axis=axis, keepdims=True)
    return (x - m) / jnp.sqrt(v + eps)

def _scatter_add(tgt, idx, src, axis=0):
    return tgt.at[idx].add(src)

def _segment_sum(src, seg, n):
    return jax.ops.segment_sum(src, seg, n)
kernel_name = 'mk_recurrent_d1_jaxref_r4_e15d0d'

def setup_inputs(seed: int=0):
    np.random.seed(seed)
    _w = jnp.asarray

    def _L0_attn_setup():
        import jax, jax.numpy as jnp
        import numpy as np
        import math
        N_EMBD = 256
        N_HEAD = 16
        HEAD_DIM = N_EMBD // N_HEAD
        BLOCK_SIZE = 512
        ROPE_BASE = 10000.0
        B, T = (4, 512)

        def _rope_cache(n_pos):
            theta = 1.0 / ROPE_BASE ** (jnp.arange(0, HEAD_DIM, 2, dtype=jnp.float32) / HEAD_DIM)
            idx_theta = jnp.arange(n_pos, dtype=jnp.float32)[:, None] * theta[None, :]
            return (jnp.cos(idx_theta), jnp.sin(idx_theta))

        def _apply_rope(x):
            cos, sin = _rope_cache(x.shape[1])
            cos = cos[None, :, None, :]
            sin = sin[None, :, None, :]
            xs = x.reshape(*x.shape[:-1], HEAD_DIM // 2, 2)
            x0, x1 = (xs[..., 0], xs[..., 1])
            out = jnp.stack([x0 * cos - x1 * sin, x1 * cos + x0 * sin], axis=-1)
            return out.reshape(x.shape)
        key = jax.random.key(seed)
        ks = jax.random.split(key, 5)
        x = jax.random.normal(ks[0], (B, T, N_EMBD), dtype=jnp.float32)
        s1 = 1.0 / math.sqrt(N_EMBD)
        W_attn = jax.random.uniform(ks[1], (N_EMBD, 3 * N_EMBD), jnp.float32, -s1, s1)
        b_attn = jax.random.uniform(ks[2], (3 * N_EMBD,), jnp.float32, -s1, s1)
        W_proj = jax.random.uniform(ks[3], (N_EMBD, N_EMBD), jnp.float32, -s1, s1)
        b_proj = jax.random.uniform(ks[4], (N_EMBD,), jnp.float32, -s1, s1)
        return {'x': x, 'W_attn': W_attn, 'b_attn': b_attn, 'W_proj': W_proj, 'b_proj': b_proj}
    _L0_attn_in = _L0_attn_setup()

    def _L0_ffn_setup():
        import jax, jax.numpy as jnp
        import numpy as np
        DIM = 256
        HIDDEN = 768
        SCALE = 1.0 / 127.0

        def _dequant(w_int, dtype):
            return w_int.astype(dtype) * jnp.asarray(SCALE, dtype)
        key = jax.random.key(seed)
        k_x, k_g, k_u, k_d = jax.random.split(key, 4)
        x = jax.random.normal(k_x, (4, 512, DIM), dtype=jnp.float32)
        w_gate = jax.random.randint(k_g, (HIDDEN, DIM), -127, 128, dtype=jnp.int32)
        w_up = jax.random.randint(k_u, (HIDDEN, DIM), -127, 128, dtype=jnp.int32)
        w_down = jax.random.randint(k_d, (DIM, HIDDEN), -127, 128, dtype=jnp.int32)
        return {'x': x, 'w_gate': w_gate, 'w_up': w_up, 'w_down': w_down}
    _L0_ffn_in = _L0_ffn_setup()
    _d = {'L0_attn_x': _L0_attn_in['x'], 'L0_attn_W_attn': _L0_attn_in['W_attn'], 'L0_attn_b_attn': _L0_attn_in['b_attn'], 'L0_attn_W_proj': _L0_attn_in['W_proj'], 'L0_attn_b_proj': _L0_attn_in['b_proj'], 'L0_ffn_w_gate': _L0_ffn_in['w_gate'], 'L0_ffn_w_up': _L0_ffn_in['w_up'], 'L0_ffn_w_down': _L0_ffn_in['w_down']}
    _x0 = _d['L0_attn_x']
    _d['L0_attn_x'] = jax.random.normal(jax.random.fold_in(jax.random.key(seed), 1), (8, 1024, 256), dtype=_x0.dtype)
    del _x0
    return _d

def reference(L0_attn_x, L0_attn_W_attn, L0_attn_b_attn, L0_attn_W_proj, L0_attn_b_proj, L0_ffn_w_gate, L0_ffn_w_up, L0_ffn_w_down):

    def _L0_attn_ref(x, W_attn, b_attn, W_proj, b_proj):
        import jax, jax.numpy as jnp
        import numpy as np
        import math
        N_EMBD = 256
        N_HEAD = 16
        HEAD_DIM = N_EMBD // N_HEAD
        BLOCK_SIZE = 512
        ROPE_BASE = 10000.0
        B, T = (4, 512)

        def _rope_cache(n_pos):
            theta = 1.0 / ROPE_BASE ** (jnp.arange(0, HEAD_DIM, 2, dtype=jnp.float32) / HEAD_DIM)
            idx_theta = jnp.arange(n_pos, dtype=jnp.float32)[:, None] * theta[None, :]
            return (jnp.cos(idx_theta), jnp.sin(idx_theta))

        def _apply_rope(x):
            cos, sin = _rope_cache(x.shape[1])
            cos = cos[None, :, None, :]
            sin = sin[None, :, None, :]
            xs = x.reshape(*x.shape[:-1], HEAD_DIM // 2, 2)
            x0, x1 = (xs[..., 0], xs[..., 1])
            out = jnp.stack([x0 * cos - x1 * sin, x1 * cos + x0 * sin], axis=-1)
            return out.reshape(x.shape)
        Bx, Tx, C = x.shape
        qkv = jnp.einsum('btc,cd->btd', x, W_attn) + b_attn
        q, k, v = jnp.split(qkv, 3, axis=2)
        q = q.reshape(Bx, Tx, N_HEAD, HEAD_DIM).transpose(0, 2, 1, 3)
        k = k.reshape(Bx, Tx, N_HEAD, HEAD_DIM).transpose(0, 2, 1, 3)
        v = v.reshape(Bx, Tx, N_HEAD, HEAD_DIM).transpose(0, 2, 1, 3)
        q = _apply_rope(q)
        k = _apply_rope(k)
        scale = 1.0 / math.sqrt(HEAD_DIM)
        att = jnp.einsum('bhqd,bhkd->bhqk', q, k) * scale
        causal = jnp.tril(jnp.ones((Tx, Tx), dtype=bool))
        att = jnp.where(causal[None, None], att, -jnp.inf)
        att = jax.nn.softmax(att, axis=-1)
        y = jnp.einsum('bhqk,bhkd->bhqd', att, v)
        y = y.transpose(0, 2, 1, 3).reshape(Bx, Tx, C)
        return jnp.einsum('btc,cd->btd', y, W_proj) + b_proj

    def _L0_ffn_ref(x, w_gate, w_up, w_down):
        import jax, jax.numpy as jnp
        import numpy as np
        DIM = 256
        HIDDEN = 768
        SCALE = 1.0 / 127.0

        def _dequant(w_int, dtype):
            return w_int.astype(dtype) * jnp.asarray(SCALE, dtype)
        wg = _dequant(w_gate, x.dtype)
        wu = _dequant(w_up, x.dtype)
        wd = _dequant(w_down, x.dtype)
        gate = jnp.einsum('bsd,hd->bsh', x, wg)
        up = jnp.einsum('bsd,hd->bsh', x, wu)
        h = jax.nn.silu(gate) * up
        return jnp.einsum('bsh,dh->bsd', h, wd)
    x = L0_attn_x
    xn = _layernorm(x, axis=-1)
    s = _L0_attn_ref(xn, L0_attn_W_attn, L0_attn_b_attn, L0_attn_W_proj, L0_attn_b_proj)
    g = _silu(_L0_ffn_ref(xn, L0_ffn_w_gate, L0_ffn_w_up, L0_ffn_w_down))
    x = x + s * g
    return x

_drawn_inputs = setup_inputs


def setup_inputs(seed=0):
    import zlib

    import numpy as np

    out = dict(_drawn_inputs(seed))
    spreads = {}
    factors = {}
    for name, (base, spread) in spreads.items():
        noise = np.random.default_rng([zlib.crc32(name.encode()), seed]).standard_normal(out[name].shape)
        drawn = base * np.exp(spread * noise) if base else spread * noise
        out[name] = jnp.asarray(drawn.astype(out[name].dtype))
    for name, factor in factors.items():
        out[name] = (out[name] * factor).astype(out[name].dtype)
    return out
```

```python
import numpy as np
import concourse.bass as bass
from concourse import mybir
from contextlib import ExitStack

B, T, C, H, D, HID = 8, 1024, 256, 16, 16, 768
P = 128
TT = T // P
GROUPS, GH = 4, 4
STEPS = 12
CH = 512
PARTS = 6
MROW = PARTS * D
LEAD = 16
NST, NMX, NP = 3, 2, 2 * GH
Q_PART = (0, 0, 1, 0, 1, 2)
K_PART = (0, 1, 0, 2, 1, 0)
XS = 2048.0
QSCALE = 1.0 / 127.0
EPS = 1e-5
NEG = -3.0e38

BLOCKS = [(0, k) for k in range(4)] + [(1, k) for k in range(8)]


def width(n):
    qc, kb = BLOCKS[n]
    return (qc + 1) * CH - max(qc * CH, kb * P)


def is_diag(n):
    qc, kb = BLOCKS[n]
    return kb >= 4 * qc


def pieces(s):
    if s < 4:
        return [(j, s, 0, P * (s + 1), True) for j in range(GH)]
    t, sub = 4 + (s - 4) // 2, (s - 4) % 2
    out = []
    for j in (2 * sub, 2 * sub + 1):
        out += [(j, t, 0, CH, False), (j, t, CH, P * (t - 3), True)]
    return out


TASKS = {
    (0, 1): [("QK", 1, 0, 0)],
    (0, 2): [("YT", 3, 1), ("QK", 1, 0, 1)],
    (0, 3): [("QK", 1, 1, 0), ("QK", 1, 1, 1)],
    (0, 4): [("FIN_T", 0), ("FIN_T", 1)],
    (0, 5): [("FIN_P", 0), ("FIN_T", 2)],
    (0, 6): [("YT", 0, 0), ("FIN_P", 1), ("FIN_O", 0)],
    (0, 7): [("FIN_T", 3), ("FIN_P", 2), ("FIN_O", 1)],
    (0, 8): [("MT", 1), ("FIN_P", 3), ("FIN_O", 2)],
    (0, 9): [("FIN_O", 3), ("UP", 0, 0)],
    (0, 10): [("V", 1, 0), ("UP", 0, 1)],
    (0, 11): [("V", 1, 1), ("UP", 0, 2)],
    (1, 0): [("UP", 0, 3)],
    (1, 1): [("UP", 0, 4)],
    (1, 2): [("YT", 0, 1), ("UP", 0, 5)],
    (1, 3): [("LNS", 0), ("DN", 0, 0), ("DN", 0, 1)],
    (1, 4): [("LNS", 1), ("UP", 1, 0)],
    (1, 5): [("LNS", 2), ("UP", 1, 1)],
    (1, 6): [("LNS", 3), ("YT", 1, 0), ("UP", 1, 2)],
    (1, 7): [("LNR",), ("UP", 1, 3)],
    (1, 8): [("LNA", 0), ("MT", 2), ("UP", 1, 4)],
    (1, 9): [("LNA", 1), ("UP", 1, 5)],
    (1, 10): [("LNA", 2)],
    (1, 11): [("LNA", 3), ("DN", 1, 0), ("DN", 1, 1)],
    (2, 0): [("TX", 0, 0), ("TX", 1, 0), ("TX", 0, 1), ("TX", 1, 1)],
    (2, 1): [("QK", 0, 0, 0), ("QK", 0, 0, 1)],
    (2, 2): [("YT", 1, 1), ("QK", 0, 1, 0)],
    (2, 3): [("QK", 0, 1, 1)],
    (2, 6): [("YT", 2, 0)],
    (2, 8): [("MT", 3)],
    (2, 9): [("V", 0, 0)],
    (2, 10): [("V", 0, 1)],
    (3, 2): [("YT", 2, 1)],
    (3, 6): [("YT", 3, 0)],
    (3, 8): [("MT", 0)],
}
PRO = ([("LNS", p) for p in range(4)] + [("LNR",)] + [("LNA", p) for p in range(4)]
       + [("TX", 0, 0), ("TX", 1, 0), ("TX", 0, 1), ("TX", 1, 1)]
       + [("QK", 0, 0, 0), ("QK", 0, 0, 1), ("QK", 0, 1, 0), ("QK", 0, 1, 1), ("V", 0, 0), ("V", 0, 1)]
       + [("MT", 0)])
EPI = ([("YT", 3, 1), ("FIN_T", 0), ("FIN_T", 1)]
       + [("FIN_P", 0), ("FIN_T", 2), ("FIN_P", 1), ("FIN_O", 0), ("FIN_T", 3), ("FIN_P", 2), ("FIN_O", 1)]
       + [("FIN_P", 3), ("FIN_O", 2), ("FIN_O", 3)])


def of_next(task):
    return task[0] in ("LNS", "LNR", "LNA", "TX") or task[:2] in (("QK", 0), ("V", 0)) or task == ("MT", 0)


def of_last(g, task):
    return task[0].startswith("FIN") or (g == 0 and task == ("YT", 3, 1))


def tasks_at(kind, g, n):
    return [t for t in TASKS.get((g, n), [])
            if not (kind == "first" and of_last(g, t)) and not (kind == "last" and of_next(t))]


ORDER = {"pro": PRO, "epi": EPI}
for _kind in ("first", "mid", "last"):
    ORDER[_kind] = [t for g in range(GROUPS) for n in range(STEPS) for t in tasks_at(_kind, g, n)]


class Tally:

    def __init__(self, events):
        self.seen = {k: [e for t in ORDER[k] for e in events(k, t)] for k in ORDER}
        n = {k: len(v) for k, v in self.seen.items()}
        self.base = {"pro": 0, "first": n["pro"], "mid": n["pro"] + n["first"]}
        self.each = n["mid"]
        self.base["last"] = self.base["mid"] + (B - 2) * self.each
        self.base["epi"] = self.base["last"] + n["last"]

    def at(self, kind, i, event):
        k = self.base[kind] + self.seen[kind].index(event) + 1
        return k + (i - 1) * self.each if kind == "mid" else k


def bank_uses():
    of = {}
    for kind in ("pro", "mid", "epi"):
        n = 0
        for t in ORDER[kind]:
            names = {"UP": ("gate", "up"), "LNS": (), "LNR": (), "LNA": (), "FIN_O": ()}.get(t[0], ("",))
            for name in names:
                of[kind, t, name] = n % 2
                n += 1
    for kind in ("first", "last"):
        of.update({(kind, t, name): b for (k, t, name), b in of.items() if k == "mid" and t in ORDER[kind]})
    return of


BANK = bank_uses()
FFN_SCALE = 0.5 * QSCALE ** 3 / XS ** 2
NEWTON = 3
LN_EACH = 2 * TT + 3 + 3 * NEWTON

USES = [Tally(lambda k, t, b=b: [(t, name) for name in ("", "gate", "up") if BANK.get((k, t, name)) == b])
        for b in range(2)]
BY = {name: Tally(lambda k, t, name=name: [t] if t[0] in name.split("+") else [])
      for name in ("TX", "QK", "UP+DN", "LNA", "YT", "FIN_P", "FIN_O", "MT")}


def tanh_before(kind, i, task):
    seen = BY["UP+DN"].seen[kind]
    k = seen.index(task) - 2
    if k >= 0:
        return kind, i, seen[k]
    return None if kind == "first" else ("mid", i - 1, seen[k])


def th_buffer(kind, task):
    return BY["UP+DN"].seen[kind].index(task) % 2


def ln_number(kind, i):
    return 0 if kind == "pro" else i + 1


def diag_count(i, g, n):
    return 2 * GH * (GROUPS * i + g) + (n if n < 4 else n - 4) + 1


def wait(eng, sem, count):
    if isinstance(count, int) and count <= 0:
        return
    eng.wait_ge(sem, count)


def stand(eng, sem):
    eng.sem_inc(sem, 1)


def build_program(nc, x, w_attn, b_attn, w_proj, b_proj, w_gate_t, w_up_t, w_down_t, rope_cos, rope_sin, out):
    fp32, bf16, fp16, i32 = mybir.dt.float32, mybir.dt.bfloat16, mybir.dt.float16, mybir.dt.int32
    ALU, ACT, AX = mybir.AluOpType, mybir.ActivationFunctionType, mybir.AxisListType

    parts_dram = nc.dram_tensor("parts_scratch", (2, 2, 3, P, T), bf16).ap()
    mrow_dram = nc.dram_tensor("maxima_scratch", (GROUPS, 3 * GH, T), bf16).ap()
    bias_dram = nc.dram_tensor("bias_scratch", (1, 2 * C), fp32).ap()
    x_tiles = x.rearrange("b (t p) c -> b p t c", p=P)
    out_tiles = out.rearrange("b (t p) c -> b p t c", p=P)

    with ExitStack() as ctx:
        def sb(name, shape, dt):
            return ctx.enter_context(nc.sbuf_tensor(name, shape, dt))

        def sem(name):
            return ctx.enter_context(nc.semaphore(name))

        w_qkv = sb("w_qkv", [P, 2, 3 * C], fp32)
        w_pr = sb("w_pr", [P, 2, C], fp32)
        w_ga = sb("w_ga", [P, 2, HID], bf16)
        w_up = sb("w_up", [P, 2, HID], bf16)
        w_dn = sb("w_dn", [P, HID // P, C], fp32)
        b_row = sb("b_row", [1, 2 * C], fp32)
        b_qk = sb("b_qk", [P, 4], fp32)
        b_v = sb("b_v", [P, C], fp32)
        b_pr = sb("b_pr", [P, C], fp32)
        ident = sb("ident", [P, P], fp32)
        ident16 = sb("ident16", [P, P], bf16)
        tri = sb("tri", [P, CH], bf16)
        parts = sb("parts", [P, 2, 3, T], bf16)
        xn = parts[:, :, :, :].rearrange("p a b t -> p (a b t)")[:, 0:2 * TT * C].bitcast(fp32)\
            .rearrange("p (t c) -> p t c", c=C)
        xnT = sb("xnT", [P, 2, T], fp32)
        xh = sb("xh", [P, 2, T], fp16)
        xl = sb("xl", [P, 2, T], fp16)
        qkf = sb("qkf", [P, 2, CH], fp32)
        qkr = sb("qkr", [P, 2, CH], fp32)
        q_st = sb("q_st", [P, GROUPS, GH, T], bf16)
        k_st = sb("k_st", [P, GROUPS, GH, T], bf16)
        v_pad = sb("v_pad", [P, TT, H, D + 1], fp32)
        pexp = sb("pexp", [P, NP, CH], fp32)
        yT = sb("yT", [P, 2, CH], fp32)
        yn = sb("yn", [P, TT, C], fp32)
        ynT = sb("ynT", [P, 2, 2, 2 * P], fp32)
        yrec = sb("yrec", [P, 2, 4 * GH], fp32)
        mx_a = sb("mx_a", [P, 2, GH, TT], fp32)
        mx_b = sb("mx_b", [P, 2, GH, TT // 2], fp32)
        mx_r = sb("mx_r", [P, GH, TT], fp32)
        mx_p = sb("mx_p", [P, TT, 3, GH], bf16)
        mT = sb("mT", [3 * GH, T], bf16)
        junk = sb("junk", [P, 2, CH], bf16)
        hT = sb("hT", [P, HID // P, CH], fp32)
        th = sb("th", [P, 2, CH], fp32)
        gu = sb("gu", [P, CH], fp32)
        g2 = sb("g2", [P, TT, C], fp32)
        cosb = g2[:, 0, :].rearrange("p (a n) -> p a n", a=2)
        sinb = g2[:, 1, :].rearrange("p (a n) -> p a n", a=2)
        xo = sb("xo", [P, 2, 2, C], fp32)
        so = sb("so", [P, 2, 2 * C], fp32)
        ln6 = sb("ln6", [P, TT, 6], fp32)
        lnv = sb("lnv", [P, TT, 2], fp32)
        lne = sb("lne", [P, TT], fp32)
        lnt = sb("lnt", [P, TT], fp32)
        rstd = sb("rstd", [P, TT], fp32)
        st = ctx.enter_context(nc.psum_tensor("st", [P, NST, CH], fp32))
        mx = ctx.enter_context(nc.psum_tensor("mx", [P, NMX, CH], fp32))
        acc = ctx.enter_context(nc.psum_tensor("acc", [P, CH], fp32))
        tb = ctx.enter_context(nc.psum_tensor("tb", [P, 2, CH], fp32))

        x_in = sem("x_in")
        w_in = {n: sem("w_in_" + n) for n in ("attn", "rope", "bias", "proj", "gate", "up", "down", "rest")}
        w_ready = sem("w_ready")
        w_chain = sem("w_chain")
        b_back = sem("b_back")
        const_ready = sem("const_ready")
        ones_ready = sem("ones_ready")
        ln_chain = sem("ln_chain")
        xn_ready = sem("xn_ready")
        xT_ready = sem("xT_ready")
        task_ready = [sem(f"task_ready{b}") for b in range(2)]
        task_free = [sem(f"task_free{b}") for b in range(2)]
        qk_first = sem("qk_first")
        qk_rest = sem("qk_rest")
        qk_second = sem("qk_second")
        qk_third = sem("qk_third")
        parts_out = sem("parts_out")
        stack_in = [sem(f"stack_in{g}") for g in range(GROUPS)]
        mx_ready = sem("mx_ready")
        mx_done = sem("mx_done")
        mp_chain = sem("mp_chain")
        mrow_out = sem("mrow_out")
        mrow_in = [sem(f"mrow_in{g}") for g in range(GROUPS)]
        st_ready = sem("st_ready")
        exp_done = sem("exp_done")
        tri_done = sem("tri_done")
        pv_done = sem("pv_done")
        acc_out = sem("acc_out")
        yrec_ready = sem("yrec_ready")
        const0 = sem("const0")
        th_ready = sem("th_ready")
        so_scaled = sem("so_scaled")
        xo_in = [sem(f"xo_in{b}") for b in range(2)]
        o_ready = sem("o_ready")
        o_out = [sem(f"o_out{b}") for b in range(2)]

        dve_stand, pool_stand, sp_stand = sem("dve_stand"), sem("pool_stand"), sem("sp_stand")

        block = ctx.enter_context(nc.Block())

        def bank(kind, task, name=""):
            return BANK[kind, task, name]

        def use(kind, i, task, name=""):
            return USES[bank(kind, task, name)].at(kind, i, (task, name))

        def wait_ready(eng, kind, i, task, name=""):
            eng.wait_ge(task_ready[bank(kind, task, name)], use(kind, i, task, name))

        def wait_done(eng, kind, i, task, name=""):
            eng.wait_ge(task_free[bank(kind, task, name)], use(kind, i, task, name))

        def last_of_previous(kind, i):
            return kind, i, ("YT", 3, 1)

        def run(engine, body, prologue, epilogue):
            prologue()
            body("first", 0)
            with engine.Fori(1, B - 1) as i:
                body("mid", i)
            body("last", B - 1)
            epilogue()

        def max_steps(kind, i, g, n):
            ahead = STEPS * g + n + LEAD
            du, s = divmod(ahead, STEPS)
            if kind == "last" and du >= GROUPS:
                return None
            return 4 * i + du, du % GROUPS, s

        w_raw = {
            "gate": hT[:, 0:3, :].rearrange("p m n -> p (m n)").bitcast(i32).rearrange("p (k n) -> p k n", k=2),
            "up": hT[:, 3:6, :].rearrange("p m n -> p (m n)").bitcast(i32).rearrange("p (k n) -> p k n", k=2),
            "down": yn[:, :, :].rearrange("p t c -> p (t c)")[:, 0:6 * C].bitcast(i32)
                .rearrange("p (k n) -> p k n", k=6),
        }

        @block.sync
        def _(sp):
            def load_stack(i, g, unit):
                hf = g // 2
                sp.wait_ge(parts_out, 32 * (2 * i + hf + 1))
                stand(sp, sp_stand)
                wait(sp, st_ready, STEPS * GH * (unit - GROUPS + 1))
                for stack, part_of, which in ((q_st, Q_PART, 0), (k_st, K_PART, 1)):
                    for s in range(PARTS):
                        src = parts_dram[hf, which, part_of[s], 64 * (g % 2):64 * (g % 2) + 64, :]
                        sp.dma_start(stack[D * s:D * s + D, g, :, :],
                                     src.rearrange("(j d) n -> d j n", d=D)).then_inc(stack_in[g], 16)

            def store_parts(kind, i, hf):
                for which in range(2):
                    sp.wait_ge(qk_third, BY["QK"].at(kind, i, ("QK", hf, which, 1)))
                    sp.dma_start(parts_dram[hf, which].rearrange("a p n -> p a n"),
                                 parts[:, which, :, :]).then_inc(parts_out, 16)

            def load_x(i):
                stand(sp, sp_stand)
                sp.dma_start(xn, batch(x_tiles, i)).then_inc(x_in, 16)

            def batch(tiles, i):
                if isinstance(i, int):
                    return tiles[i]
                return tiles[bass.ds(i, 1)].rearrange("b p t c -> p (b t) c")

            def store_maxima(kind, i, g):
                wait_done(sp, kind, i, ("MT", g))
                sp.dma_start(mrow_dram[g], mT[:, :]).then_inc(mrow_out, 16)
                sp.wait_ge(mrow_out, 16 * BY["MT"].at(kind, i, ("MT", g)))
                sp.dma_start(q_st[MROW:MROW + 3, g, :, :],
                             mrow_dram[g].rearrange("(a j) n -> a j n", a=3)).then_inc(mrow_in[g], 16)

            def load_xo(kind, i, tp):
                buf = tp % 2
                wait(sp, o_out[buf], 16 * (2 * i + tp // 2))
                stand(sp, sp_stand)
                sp.dma_start(xo[:, buf, :, :], batch(x_tiles, i)[:, 2 * tp:2 * tp + 2, :]).then_inc(xo_in[buf], 16)

            def store_out(kind, i, tp, done_of):
                buf = tp % 2
                sp.wait_ge(o_ready, BY["FIN_O"].at(kind, i, ("FIN_O", tp)))
                stand(sp, sp_stand)
                sp.dma_start(batch(out_tiles, done_of)[:, 2 * tp:2 * tp + 2, :], xo[:, buf, :, :])\
                    .then_inc(o_out[buf], 16)

            def task(kind, i, g, t):
                if t == ("QK", 1, 1, 1):
                    store_parts(kind, i, 1)
                    load_stack(i, 2, 4 * i + 2)
                    load_stack(i, 3, 4 * i + 3)
                    if kind != "last":
                        load_x(i + 1)
                if t == ("QK", 0, 1, 1):
                    store_parts(kind, i, 0)
                    load_stack(i + 1, 0, 4 * i + 4)
                    load_stack(i + 1, 1, 4 * i + 5)
                if t[0] == "MT":
                    store_maxima(kind, i, t[1])
                if t[0] == "FIN_T" and t[1] < 2:
                    load_xo(kind, i - 1, t[1])
                if t[0] == "FIN_O":
                    store_out(kind, i, t[1], i - 1)
                    if t[1] < 2:
                        load_xo(kind, i - 1, t[1] + 2)

            def prologue():
                load_x(0)
                sp.dma_start(w_qkv[:, :, :], w_attn.rearrange("(k p) n -> p k n", p=P)).then_inc(w_in["attn"], 16)
                sp.dma_start(cosb, rope_cos.rearrange("p (a n) -> p a n", a=2)).then_inc(w_in["rope"], 16)
                sp.dma_start(sinb, rope_sin.rearrange("p (a n) -> p a n", a=2)).then_inc(w_in["rope"], 16)
                sp.dma_start(b_row[:, :], b_attn[:, 0:2 * C]).then_inc(w_in["bias"], 16)
                sp.wait_ge(w_ready, 2)
                sp.dma_start(bias_dram, b_row[:, :]).then_inc(b_back, 16)
                sp.wait_ge(b_back, 16)
                sp.dma_start(b_qk[:, :], bias_dram.rearrange("o (t p) -> p (o t)", p=P),
                             allow_slow_non_contiguous=True).then_inc(b_back, 16)
                sp.dma_start(b_v[:, :], b_attn[:, 2 * C:3 * C].broadcast_to([P, C])).then_inc(w_in["rest"], 16)
                sp.dma_start(b_pr[:, :], b_proj.broadcast_to([P, C])).then_inc(w_in["rest"], 16)
                sp.dma_start(w_pr[:, :, :], w_proj.rearrange("(k p) n -> p k n", p=P)).then_inc(w_in["proj"], 16)
                sp.dma_start(w_raw["gate"], w_gate_t.rearrange("(k p) n -> p k n", p=P)).then_inc(w_in["gate"], 16)
                sp.dma_start(w_raw["up"], w_up_t.rearrange("(k p) n -> p k n", p=P)).then_inc(w_in["up"], 16)
                sp.dma_start(w_raw["down"], w_down_t.rearrange("(k p) n -> p k n", p=P)).then_inc(w_in["down"], 16)
                store_parts("pro", 0, 0)
                load_stack(0, 0, 0)
                load_stack(0, 1, 1)
                store_maxima("pro", 0, 0)

            def body(kind, i):
                for g in range(GROUPS):
                    for n in range(STEPS):
                        for t in tasks_at(kind, g, n):
                            task(kind, i, g, t)

            def epilogue():
                for t in EPI:
                    task("epi", B, 0, t)
                for buf in range(2):
                    sp.wait_ge(o_out[buf], 16 * 2 * B)

            run(sp, body, prologue, epilogue)

        @block.tensor
        def _(pe):
            def take(kind, i, task, name=""):
                b = bank(kind, task, name)
                wait(pe, task_free[b], use(kind, i, task, name) - 1)
                return tb[:, b, :], task_ready[b]

            def scores(i, g, n, j):
                qc, kb = BLOCKS[n]
                w = width(n)
                index = STEPS * GH * (4 * i + g) + GH * n + j
                wait(pe, exp_done, index - NST + 1)
                if n == 0 and j == 0:
                    pe.wait_ge(mrow_in[g], 16 * (i + 1))
                q0 = (qc + 1) * CH - w
                nc.tensor.matmul(st[:, (GH * n + j) % NST, 0:w], k_st[0:MROW + 3, g, j, kb * P:(kb + 1) * P],
                                 q_st[0:MROW + 3, g, j, q0:q0 + w], start=True, stop=True).then_inc(st_ready, 1)

            def max_piece(unit, g, s, c, i_next):
                j, t, k0, w, _ = pieces(s)[c]
                if s == 0 and c == 0:
                    pe.wait_ge(stack_in[g], 16 * 2 * PARTS * (i_next + 1))
                index = (STEPS * unit + s) * GH + c
                wait(pe, mx_done, index - NMX + 1)
                nc.tensor.matmul(mx[:, c % NMX, 0:w], q_st[0:MROW, g, j, t * P:(t + 1) * P],
                                 k_st[0:MROW, g, j, k0:k0 + w], start=True, stop=True).then_inc(mx_ready, 1)

            def values(i, g, n):
                qc, kb = BLOCKS[n]
                w = width(n)
                if is_diag(n):
                    pe.wait_ge(tri_done, diag_count(i, g, n))
                else:
                    pe.wait_ge(exp_done, GH * (STEPS * (4 * i + g) + n + 1))
                if kb == 0:
                    wait(pe, acc_out, 2 * (4 * i + g) + qc)
                for j in range(GH):
                    mm = nc.tensor.matmul(acc[32 * j:32 * j + D + 1, CH - w:CH], v_pad[:, kb, GH * g + j, :],
                                          pexp[:, GH * (n % 2) + j, 0:w],
                                          start=kb == 0, stop=kb == 4 * qc + 3)
                mm.then_inc(pv_done, 1)

            def task(kind, i, g, t):
                if t[0] == "TX":
                    _, kt, c = t
                    pe.wait_ge(xn_ready, BY["LNA"].at(kind, i, ("LNA", 2 * c + 1)))
                    dst, ready = take(kind, i, t)
                    for tt in range(4):
                        mm = nc.tensor.transpose(dst[:, tt * P:(tt + 1) * P],
                                                 xn[:, 4 * c + tt, kt * P:(kt + 1) * P], ident[:, :])
                    mm.then_inc(ready, 1)
                if t[0] == "QK":
                    _, hf, which, c = t
                    if hf == 0 and which == 0 and c == 0:
                        pe.wait_ge(xT_ready, BY["TX"].at(kind, i, ("TX", 1, 1)))
                    dst, ready = take(kind, i, t)
                    col = which * C + hf * P
                    for kt in range(2):
                        mm = nc.tensor.matmul(dst, w_qkv[:, kt, col:col + P], xnT[:, kt, c * CH:(c + 1) * CH],
                                              start=kt == 0, stop=kt == 1)
                    mm.then_inc(ready, 1)
                if t[0] == "V":
                    _, hf, tq = t
                    dst, ready = take(kind, i, t)
                    for tt in range(4):
                        for kt in range(2):
                            mm = nc.tensor.matmul(dst[:, tt * P:(tt + 1) * P],
                                                  xnT[:, kt, (4 * tq + tt) * P:(4 * tq + tt + 1) * P],
                                                  w_qkv[:, kt, 2 * C + hf * P:2 * C + hf * P + P],
                                                  start=kt == 0, stop=kt == 1)
                    mm.then_inc(ready, 1)
                if t[0] == "UP":
                    _, c, m = t
                    for name, w in (("gate", w_ga), ("up", w_up)):
                        dst, ready = take(kind, i, t, name)
                        for kt in range(2):
                            for xpart in (xh, xl):
                                mm = nc.tensor.matmul(dst, w[:, kt, m * P:(m + 1) * P],
                                                      xpart[:, kt, c * CH:(c + 1) * CH],
                                                      start=kt == 0 and xpart is xh, stop=kt == 1 and xpart is xl)
                        mm.then_inc(ready, 1)
                if t[0] == "DN":
                    _, c, tp = t
                    if tp == 0:
                        wait_done(pe, kind, i, ("UP", c, HID // P - 1), "up")
                    dst, ready = take(kind, i, t)
                    for t2 in range(2):
                        for m in range(HID // P):
                            mm = nc.tensor.matmul(dst[:, t2 * C:(t2 + 1) * C],
                                                  hT[:, m, (2 * tp + t2) * P:(2 * tp + t2 + 1) * P],
                                                  w_dn[:, m, :], start=m == 0, stop=m == HID // P - 1)
                    mm.then_inc(ready, 1)
                if t[0] == "YT":
                    _, yg, qc = t
                    unit_i = i - 1 if (yg, qc) == (3, 1) else i
                    pe.wait_ge(acc_out, 2 * (4 * unit_i + yg) + qc + 1)
                    dst, ready = take(kind, i, t)
                    for tt in range(4):
                        mm = nc.tensor.transpose(dst[:, tt * P:(tt + 1) * P], yT[:, qc, tt * P:(tt + 1) * P],
                                                 ident[:, :])
                    mm.then_inc(ready, 1)
                if t[0] == "FIN_T":
                    _, tp = t
                    if tp == 0:
                        wait_done(pe, kind, i, ("YT", 3, 1))
                    dst, ready = take(kind, i, t)
                    for kt in range(2):
                        for t2 in range(2):
                            mm = nc.tensor.transpose(dst[:, kt * 2 * P + t2 * P:kt * 2 * P + (t2 + 1) * P],
                                                     yn[:, 2 * tp + t2, kt * P:(kt + 1) * P], ident[:, :])
                    mm.then_inc(ready, 1)
                if t[0] == "FIN_P":
                    _, tp = t
                    wait_done(pe, kind, i, ("FIN_T", tp))
                    dst, ready = take(kind, i, t)
                    for t2 in range(2):
                        for kt in range(2):
                            mm = nc.tensor.matmul(dst[:, t2 * C:(t2 + 1) * C],
                                                  ynT[:, tp % 2, kt, t2 * P:(t2 + 1) * P], w_pr[:, kt, :],
                                                  start=kt == 0, stop=kt == 1)
                    mm.then_inc(ready, 1)
                if t[0] == "MT":
                    pe.wait_ge(mp_chain, 5 * BY["MT"].at(kind, i, t))
                    dst, ready = take(kind, i, t)
                    for tt in range(TT):
                        mm = nc.tensor.transpose(dst[0:3 * GH, :].bitcast(bf16)[:, tt * P:(tt + 1) * P],
                                                 mx_p[:, tt, :, :].rearrange("p a j -> p (a j)"), ident16[:, :])
                    mm.then_inc(ready, 1)

            def prologue():
                pe.wait_ge(const_ready, 3)
                for t in PRO[:-1]:
                    if t == ("QK", 0, 0, 0):
                        pe.wait_ge(w_ready, 1)
                    task("pro", 0, 0, t)
                for ahead in range(LEAD):
                    unit, s = divmod(ahead, STEPS)
                    for c in range(GH):
                        max_piece(unit, unit, s, c, 0)
                    if ahead == STEPS:
                        task("pro", 0, 0, ("MT", 0))
                pe.wait_ge(w_ready, 5)
                pe.wait_ge(w_in["proj"], 16)
                for tq in range(2):
                    wait_done(pe, "pro", 0, ("V", 0, tq))

            def body(kind, i):
                for g in range(GROUPS):
                    for n in range(STEPS):
                        ahead = max_steps(kind, i, g, n)
                        i_next = i + (STEPS * g + n + LEAD) // (STEPS * GROUPS)
                        if ahead:
                            unit, mg, s = ahead
                        for half in range(2):
                            for j in (2 * half, 2 * half + 1):
                                scores(i, g, n, j)
                            if half == 1:
                                if (g, n) != (0, 0):
                                    values(i, *divmod(STEPS * g + n - 1, STEPS))
                                elif kind != "first":
                                    values(i - 1, GROUPS - 1, STEPS - 1)
                            if ahead:
                                for c in (2 * half, 2 * half + 1):
                                    max_piece(unit, mg, s, c, i_next)
                        for t in tasks_at(kind, g, n):
                            task(kind, i, g, t)

            def epilogue():
                values(B - 1, GROUPS - 1, STEPS - 1)
                for t in EPI:
                    task("epi", B, 0, t)

            run(pe, body, prologue, epilogue)

        @block.scalar
        def _(act):
            def exps(i, g, n):
                w = width(n)
                for j in range(GH):
                    index = STEPS * GH * (4 * i + g) + GH * n + j
                    if j == 0:
                        wait(act, pv_done, STEPS * (4 * i + g) + n - 1)
                    act.wait_ge(st_ready, index + 1)
                    nc.scalar.activation(pexp[:, GH * (n % 2) + j, 0:w], st[:, (GH * n + j) % NST, 0:w], ACT.Exp,
                                         scale=1.0 / np.sqrt(D)).then_inc(exp_done, 1)

            def copy_acc(i, g, qc):
                act.wait_ge(pv_done, STEPS * (4 * i + g) + (4 if qc == 0 else STEPS))
                nc.scalar.activation(yT[:, qc, :], acc[:, :], ACT.Copy).then_inc(acc_out, 1)

            def task(kind, i, g, t):
                if t[0] == "TX":
                    _, kt, c = t
                    wait_ready(act, kind, i, t)
                    src = tb[:, bank(kind, t), :]
                    nc.scalar.activation(xnT[:, kt, c * CH:(c + 1) * CH], src, ACT.Copy)
                    nc.scalar.activation(xh[:, kt, c * CH:(c + 1) * CH], src, ACT.Copy, scale=XS)\
                        .then_inc(xT_ready, 1)
                if t[0] == "QK":
                    _, hf, which, c = t
                    k = BY["QK"].at(kind, i, t)
                    src = tb[:, bank(kind, t), :]
                    bias = b_qk[:, 2 * which + hf:2 * which + hf + 1]
                    wait_ready(act, kind, i, t)
                    wait(act, qk_rest, k - 2)
                    nc.scalar.activation(qkf[:, c, :], src, ACT.Identity, bias=bias)
                    if kind != "pro":
                        act.wait_ge(parts_out, 32 * (2 * i + 2 - hf))
                    nc.scalar.activation(parts[:, which, 0, c * CH:(c + 1) * CH], src, ACT.Identity, bias=bias)\
                        .then_inc(task_free[bank(kind, t)], 1)
                if t[0] == "UP":
                    _, c, m = t
                    wait_ready(act, kind, i, t, "gate")
                    wait_th(kind, i, t)
                    nc.scalar.activation(th[:, th_buffer(kind, t), :], tb[:, bank(kind, t, "gate"), :],
                                         ACT.Tanh, scale=0.5 * QSCALE / XS).then_inc(th_ready, 1)
                if t[0] == "DN":
                    wait_ready(act, kind, i, t)
                    wait_th(kind, i, t)
                    nc.scalar.activation(th[:, th_buffer(kind, t), :], tb[:, bank(kind, t), :],
                                         ACT.Tanh, scale=0.5 * FFN_SCALE).then_inc(th_ready, 1)
                if t[0] == "FIN_T":
                    _, tp = t
                    wait_ready(act, kind, i, t)
                    b = bank(kind, t)
                    nc.scalar.activation(ynT[:, tp % 2, :, :], tb[:, b, :].rearrange("p (k n) -> p k n", k=2),
                                         ACT.Copy).then_inc(task_free[b], 1)
                if t[0] == "MT":
                    k = BY["MT"].at(kind, i, t)
                    b = bank(kind, t)
                    wait_ready(act, kind, i, t)
                    wait(act, mrow_out, 16 * (k - 1))
                    nc.scalar.activation(mT[:, :], tb[0:3 * GH, b, :].bitcast(bf16), ACT.Copy)\
                        .then_inc(task_free[b], 1)

            def wait_th(kind, i, t):
                before = tanh_before(kind, i, t)
                if before:
                    wait_done(act, *before, "gate" if before[2][0] == "UP" else "")

            def prologue():
                act.wait_ge(b_back, 32)
                for t in PRO:
                    task("pro", 0, 0, t)

            def body(kind, i):
                for g in range(GROUPS):
                    for n in range(STEPS):
                        if n == 0 and (g > 0 or kind != "first"):
                            exps(i, g, n)
                            copy_acc(i if g else i - 1, (g - 1) % GROUPS, 1)
                        else:
                            exps(i, g, n)
                        if n == 4:
                            copy_acc(i, g, 0)
                        for t in tasks_at(kind, g, n):
                            task(kind, i, g, t)

            def epilogue():
                copy_acc(B - 1, GROUPS - 1, 1)
                for t in EPI:
                    task("epi", B, 0, t)

            run(act, body, prologue, epilogue)

        @block.vector
        def _(dve):
            def max_take(unit, g, s):
                par = g % 2
                for c, (j, t, k0, w, diag) in enumerate(pieces(s)):
                    index = (STEPS * unit + s) * GH + c
                    dve.wait_ge(mx_ready, index + 1)
                    dst = mx_b[:, par, j, t - 4:t - 3] if k0 else mx_a[:, par, j, t:t + 1]
                    src = mx[:, c % NMX, 0:w]
                    if diag:
                        wait(dve, mx_done, index - 1)
                        stand(dve, dve_stand)
                        nc.vector.tensor_tensor_reduce(out=junk[:, c % 2, 0:w], in0=src, in1=tri[:, CH - w:CH],
                                                       scale=1.0, scalar=NEG, op0=ALU.add, op1=ALU.max,
                                                       accum_out=dst).then_inc(mx_done, 1)
                    else:
                        nc.vector.reduce_max(dst, src, AX.X).then_inc(mx_done, 1)

            def mp_step(ins, count):
                ins.then_inc(mp_chain, 1)
                dve.wait_ge(mp_chain, count)

            def split_maxima(kind, i, t, unit):
                par = t[1] % 2
                base = 5 * (BY["MT"].at(kind, i, t) - 1)
                m = mx_a[:, par, :, :]
                m_t = mx_a[:, par, :, :].rearrange("p j t -> p t j")
                r_t = mx_r[:, :, :].rearrange("p j t -> p t j")
                dve.wait_ge(mx_done, STEPS * GH * (unit + 1))
                mp_step(nc.vector.tensor_tensor(m[:, :, 4:8], m[:, :, 4:8], mx_b[:, par, :, :], ALU.max), base + 1)
                wait(dve, mrow_out, 16 * (BY["MT"].at(kind, i, t) - 1))
                mp_step(nc.vector.tensor_scalar(mx_p[:, :, 0, :], m_t, -1.0, None, ALU.mult), base + 2)
                mp_step(nc.vector.scalar_tensor_tensor(out=r_t, in0=m_t, scalar=-1.0, in1=mx_p[:, :, 0, :],
                                                       op0=ALU.mult, op1=ALU.subtract), base + 3)
                mp_step(nc.vector.tensor_copy(mx_p[:, :, 1, :], r_t), base + 4)
                nc.vector.tensor_tensor(mx_p[:, :, 2, :], r_t, mx_p[:, :, 1, :], ALU.subtract).then_inc(mp_chain, 1)

            def ln_step(ins, kind, i, k):
                ins.then_inc(ln_chain, 1)
                dve.wait_ge(ln_chain, LN_EACH * ln_number(kind, i) + k)

            def task(kind, i, g, t):
                if t[0] == "LNS":
                    _, p = t
                    if p == 0:
                        dve.wait_ge(x_in, 16 * (ln_number(kind, i) + 1))
                    for e in range(2):
                        tt = 2 * p + e
                        ln_step(nc.vector.bn_stats(ln6[:, tt, :], xn[:, tt, :]), kind, i, 2 * tt + 1)
                        stand(dve, dve_stand)
                        ln_step(nc.vector.bn_aggr(lnv[:, tt, :], ln6[:, tt, :]), kind, i, 2 * tt + 2)
                if t[0] == "LNR":
                    k = 2 * TT
                    ln_step(nc.vector.tensor_scalar(lne[:, :], lnv[:, :, 1], EPS, None, ALU.add), kind, i, k + 1)
                    ln_step(nc.vector.tensor_scalar(rstd[:, :].bitcast(i32), lne[:, :].bitcast(i32), 1, None,
                                                    ALU.arith_shift_right), kind, i, k + 2)
                    ln_step(nc.vector.tensor_scalar(rstd[:, :].bitcast(i32), rstd[:, :].bitcast(i32), -1.0,
                                                    float(0x5F3759DF), ALU.mult, ALU.add), kind, i, k + 3)
                    for it in range(NEWTON):
                        k = 2 * TT + 3 + 3 * it
                        ln_step(nc.vector.tensor_tensor(lnt[:, :], rstd[:, :], rstd[:, :], ALU.mult), kind, i, k + 1)
                        ln_step(nc.vector.scalar_tensor_tensor(out=lnt[:, :], in0=lnt[:, :], scalar=-0.5,
                                                               in1=lne[:, :], op0=ALU.mult, op1=ALU.mult),
                                kind, i, k + 2)
                        ln_step(nc.vector.scalar_tensor_tensor(out=rstd[:, :], in0=lnt[:, :], scalar=1.5,
                                                               in1=rstd[:, :], op0=ALU.add, op1=ALU.mult),
                                kind, i, k + 3)
                if t[0] == "LNA":
                    _, p = t
                    for e in range(2):
                        tt = 2 * p + e
                        ins = nc.vector.tensor_scalar(xn[:, tt, :], xn[:, tt, :], lnv[:, tt, 0:1], rstd[:, tt:tt + 1],
                                                      ALU.subtract, ALU.mult)
                    ins.then_inc(xn_ready, 1)
                if t[0] == "TX":
                    _, kt, c = t
                    b = bank(kind, t)
                    dve.wait_ge(xT_ready, BY["TX"].at(kind, i, t))
                    nc.vector.scalar_tensor_tensor(out=xl[:, kt, c * CH:(c + 1) * CH], in0=tb[:, b, :], scalar=XS,
                                                   in1=xh[:, kt, c * CH:(c + 1) * CH], op0=ALU.mult,
                                                   op1=ALU.subtract).then_inc(task_free[b], 1)
                if t[0] == "QK":
                    _, hf, which, c = t
                    k = BY["QK"].at(kind, i, t)
                    wait_done(dve, kind, i, t)
                    wait(dve, qk_third, k - 2)
                    part = parts[:, which, :, c * CH:(c + 1) * CH]
                    nc.vector.tensor_tensor(qkr[:, c, :], qkf[:, c, :], part[:, 0, :], ALU.subtract)\
                        .then_inc(qk_rest, 1)
                    dve.wait_ge(qk_rest, k)
                    nc.vector.tensor_copy(part[:, 1, :], qkr[:, c, :]).then_inc(qk_second, 1)
                if t[0] == "V":
                    _, hf, tq = t
                    b = bank(kind, t)
                    wait_ready(dve, kind, i, t)
                    nc.vector.tensor_tensor(
                        v_pad[:, 4 * tq:4 * tq + 4, 8 * hf:8 * hf + 8, 0:D],
                        tb[:, b, :].rearrange("p (t h d) -> p t h d", t=4, d=D),
                        b_v[:, hf * P:(hf + 1) * P].rearrange("p (o h d) -> p o h d", o=1, d=D)
                        .broadcast_to([P, 4, 8, D]), ALU.add).then_inc(task_free[b], 1)
                if t[0] == "UP":
                    _, c, m = t
                    k = BY["UP+DN"].at(kind, i, t)
                    ba, bb = bank(kind, t, "gate"), bank(kind, t, "up")
                    dve.wait_ge(th_ready, k)
                    nc.vector.scalar_tensor_tensor(out=gu[:, :], in0=th[:, th_buffer(kind, t), :], scalar=1.0,
                                                   in1=tb[:, ba, :], op0=ALU.add, op1=ALU.mult)\
                        .then_inc(task_free[ba], 1)
                    wait_done(dve, kind, i, t, "gate")
                    wait_ready(dve, kind, i, t, "up")
                    nc.vector.tensor_tensor(hT[:, m, :], gu[:, :], tb[:, bb, :], ALU.mult)\
                        .then_inc(task_free[bb], 1)
                if t[0] == "DN":
                    _, c, tp = t
                    b = bank(kind, t)
                    k = BY["UP+DN"].at(kind, i, t)
                    dve.wait_ge(th_ready, k)
                    if kind != "first" and (c, tp) == (0, 0):
                        dve.wait_ge(so_scaled, BY["FIN_P"].at(kind, i, ("FIN_P", 3)))
                    nc.vector.scalar_tensor_tensor(
                        out=g2[:, 4 * c + 2 * tp:4 * c + 2 * tp + 2, :].rearrange("p t c -> p (t c)"),
                        in0=th[:, th_buffer(kind, t), :], scalar=1.0, in1=tb[:, b, :],
                        op0=ALU.add, op1=ALU.mult).then_inc(task_free[b], 1)
                if t[0] == "YT":
                    _, yg, qc = t
                    b = bank(kind, t)
                    k = BY["YT"].at(kind, i, t)
                    wait_ready(dve, kind, i, t)
                    y4 = tb[:, b, :].rearrange("p (t j r) -> p t j r", t=4, r=32)
                    nc.vector.reciprocal(yrec[:, qc, :].rearrange("p (t j o) -> p t j o", t=4, o=1),
                                         y4[:, :, :, D:D + 1]).then_inc(yrec_ready, 1)
                    dve.wait_ge(yrec_ready, k)
                    nc.vector.tensor_tensor(
                        yn[:, 4 * qc:4 * qc + 4, yg * 64:yg * 64 + 64].rearrange("p t (j d) -> p t j d", d=D),
                        y4[:, :, :, 0:D],
                        yrec[:, qc, :].rearrange("p (t j o) -> p t j o", t=4, o=1).broadcast_to([P, 4, GH, D]),
                        ALU.mult).then_inc(task_free[b], 1)
                if t[0] == "FIN_P":
                    _, tp = t
                    b = bank(kind, t)
                    k = BY["FIN_P"].at(kind, i, t)
                    wait_ready(dve, kind, i, t)
                    if tp >= 2:
                        dve.wait_ge(o_ready, k - 2)
                    nc.vector.tensor_tensor(so[:, tp % 2, :].rearrange("p (t c) -> p t c", t=2),
                                            tb[:, b, :].rearrange("p (t c) -> p t c", t=2),
                                            b_pr[:, :].rearrange("p (o c) -> p o c", o=1).broadcast_to([P, 2, C]),
                                            ALU.add).then_inc(task_free[b], 1)
                if t[0] == "FIN_O":
                    _, tp = t
                    k = BY["FIN_O"].at(kind, i, t)
                    dve.wait_ge(so_scaled, k)
                    dve.wait_ge(xo_in[tp % 2], 16 * (2 * (i - 1) + tp // 2 + 1))
                    o = xo[:, tp % 2, :, :].rearrange("p t c -> p (t c)")
                    nc.vector.scalar_tensor_tensor(out=o, in0=so[:, tp % 2, :], scalar=0.5 * FFN_SCALE, in1=o,
                                                   op0=ALU.mult, op1=ALU.add).then_inc(o_ready, 1)

            def turn(we, wo, cos, sin, tmp, count):
                for dst, a, b in ((tmp[0], we, cos), (tmp[1], wo, sin), (tmp[2], wo, cos), (tmp[3], we, sin)):
                    last = nc.vector.tensor_tensor(dst, a, b, ALU.mult)
                last.then_inc(w_chain, 1)
                dve.wait_ge(w_chain, count)
                nc.vector.tensor_tensor(we, tmp[0], tmp[1], ALU.subtract)
                return nc.vector.tensor_tensor(wo, tmp[2], tmp[3], ALU.add)

            def prologue():
                nc.vector.memset(acc[:, :], 0.0)
                for t in PRO[:9]:
                    task("pro", 0, 0, t)
                dve.wait_ge(w_in["rope"], 32)
                dve.wait_ge(w_in["attn"], 16)
                wv = w_qkv[:, :, 0:2 * C].rearrange("p k (n two) -> p k n two", two=2)
                cos, sin = (g2[:, k:k + 1, :] for k in range(2))
                tmp = [pexp[:, k, :].rearrange("p (k n) -> p k n", k=2) for k in range(4)]
                turn(wv[:, :, :, 0], wv[:, :, :, 1], cos.broadcast_to([P, 2, C]), sin.broadcast_to([P, 2, C]),
                     tmp, 1).then_inc(w_ready, 1)
                dve.wait_ge(w_in["bias"], 16)
                bv = b_row[:, :].rearrange("p (n two) -> p n two", two=2)
                tmp = [pexp[0:1, 4 + k, 0:C] for k in range(4)]
                turn(bv[:, :, 0], bv[:, :, 1], cos[0:1, 0, :], sin[0:1, 0, :], tmp, 2).then_inc(w_ready, 1)
                for t in PRO[9:-1]:
                    if t[0] == "V" and t[2] == 0:
                        dve.wait_ge(w_in["rest"], 32)
                        dve.wait_ge(ones_ready, 2)
                    task("pro", 0, 0, t)
                dve.wait_ge(w_in["gate"], 16)
                nc.vector.tensor_copy(w_ga[:, :, :], w_raw["gate"]).then_inc(w_ready, 1)
                dve.wait_ge(w_in["up"], 16)
                nc.vector.tensor_copy(w_up[:, :, :], w_raw["up"]).then_inc(w_ready, 1)
                dve.wait_ge(w_in["down"], 16)
                nc.vector.tensor_copy(w_dn[:, :, :], w_raw["down"]).then_inc(w_ready, 1)
                dve.wait_ge(const_ready, 4)
                for ahead in range(LEAD):
                    unit, s = divmod(ahead, STEPS)
                    if ahead == STEPS:
                        split_maxima("pro", 0, ("MT", 0), 0)
                    max_take(unit, unit, s)
                dve.wait_ge(w_ready, 5)

            def body(kind, i):
                for g in range(GROUPS):
                    for n in range(STEPS):
                        ahead = max_steps(kind, i, g, n)
                        for t in tasks_at(kind, g, n):
                            if t[0] == "MT":
                                split_maxima(kind, i, t, 4 * i + g + 1)
                        if ahead:
                            max_take(*ahead)
                        for t in tasks_at(kind, g, n):
                            task(kind, i, g, t)

            def epilogue():
                for t in EPI:
                    task("epi", B, 0, t)

            run(dve, body, prologue, epilogue)

        @block.gpsimd
        def _(pool):
            def mask(i, g, n):
                pool.wait_ge(exp_done, GH * (STEPS * (4 * i + g) + n + 1))
                stand(pool, pool_stand)
                t = pexp[:, GH * (n % 2):GH * (n % 2) + GH, 0:P]
                nc.gpsimd.affine_select(out=t, in_=t, compare_op=ALU.is_ge, fill=0.0, base=0,
                                        pattern=[[0, GH], [1, P]], channel_multiplier=-1).then_inc(tri_done, 1)

            def task(kind, i, g, t):
                if t[0] == "QK":
                    _, hf, which, c = t
                    pool.wait_ge(qk_second, BY["QK"].at(kind, i, t))
                    part = parts[:, which, :, c * CH:(c + 1) * CH]
                    nc.gpsimd.tensor_tensor(part[:, 2, :], qkr[:, c, :], part[:, 1, :], ALU.subtract)\
                        .then_inc(qk_third, 1)
                if t[0] == "FIN_P":
                    _, tp = t
                    wait_done(pool, kind, i, t)
                    s = so[:, tp % 2, :]
                    nc.gpsimd.tensor_tensor(s, s, g2[:, 2 * tp:2 * tp + 2, :].rearrange("p t c -> p (t c)"),
                                            ALU.mult).then_inc(so_scaled, 1)

            def prologue():
                pool.memset(ident[:, :], 0.0).then_inc(const0, 1)
                pool.memset(ident16[:, :], 0.0).then_inc(const0, 1)
                pool.memset(tri[:, :], 0.0).then_inc(const0, 1)
                pool.wait_ge(const0, 3)
                for m in (ident, ident16):
                    pool.affine_select(out=m[:, :], in_=m[:, :], compare_op=ALU.not_equal, fill=1.0, base=0,
                                       pattern=[[-1, P]], channel_multiplier=1).then_inc(const_ready, 1)
                pool.wait_ge(const_ready, 2)
                pool.memset(k_st[MROW:MROW + 3, :, :, :].rearrange("p g j n -> p (g j n)").bitcast(fp32),
                            float(np.uint32(0x3F803F80).view(np.float32))).then_inc(const_ready, 1)
                pool.wait_ge(const_ready, 3)
                pool.affine_select(out=tri[:, CH - P:CH], in_=tri[:, CH - P:CH], compare_op=ALU.is_ge, fill=NEG,
                                   base=0, pattern=[[-1, P]], channel_multiplier=1).then_inc(const_ready, 1)
                pool.memset(v_pad[:, :, 0:8, D:D + 1], 1.0).then_inc(ones_ready, 1)
                pool.memset(v_pad[:, :, 8:16, D:D + 1], 1.0).then_inc(ones_ready, 1)
                for t in PRO:
                    task("pro", 0, 0, t)

            def body(kind, i):
                for g in range(GROUPS):
                    for n in range(STEPS):
                        if is_diag(n):
                            mask(i, g, n)
                        for t in tasks_at(kind, g, n):
                            task(kind, i, g, t)

            def epilogue():
                for t in EPI:
                    task("epi", B, 0, t)

            run(pool, body, prologue, epilogue)


_OUT = ((B, T, C), "float32")


def kernel(**inputs):
    import concourse.bacc as _bacc
    from concourse import mybir as _mybir
    from concourse.bass_utils import run_bass_kernel_spmd as _run

    theta = 1.0 / np.power(np.float32(10000.0), np.arange(0, D, 2, dtype=np.float32) / np.float32(D))
    angle = (np.arange(H, dtype=np.float32)[:, None] * theta.astype(np.float32)[None, :]).astype(np.float32)
    tables = {n: np.ascontiguousarray(np.broadcast_to(np.tile(f(angle).astype(np.float32).reshape(1, -1), (1, 2)),
                                                      (P, C)))
              for n, f in (("rope_cos", np.cos), ("rope_sin", np.sin))}
    arrays = {
        "x": np.asarray(inputs["L0_attn_x"]),
        "w_attn": np.asarray(inputs["L0_attn_W_attn"]),
        "b_attn": np.asarray(inputs["L0_attn_b_attn"]).reshape(1, -1),
        "w_proj": np.asarray(inputs["L0_attn_W_proj"]),
        "b_proj": np.asarray(inputs["L0_attn_b_proj"]).reshape(1, -1),
        "w_gate_t": np.asarray(inputs["L0_ffn_w_gate"]).T,
        "w_up_t": np.asarray(inputs["L0_ffn_w_up"]).T,
        "w_down_t": np.asarray(inputs["L0_ffn_w_down"]).T,
        **tables,
    }
    nc = _bacc.Bacc("TRN2", target_bir_lowering=False, num_devices=1)
    maps, args = {}, []
    for name, a in arrays.items():
        a = np.ascontiguousarray(a)
        maps[f"in_{name}"] = a
        args.append(nc.dram_tensor(f"in_{name}", a.shape, _mybir.dt.from_np(a.dtype), kind="ExternalInput").ap())
    shape, dtype = _OUT
    out = nc.dram_tensor("out_0", shape, _mybir.dt.from_np(np.dtype(dtype)), kind="ExternalOutput").ap()
    build_program(nc, *args, out)
    r = _run(nc, [maps], core_ids=[0])
    return r.results[0]["out_0"]
```

```python
import numpy as np
import concourse.bass as bass
from concourse import mybir
from contextlib import ExitStack

B, T, C, H, D, HID = 8, 1024, 256, 16, 16, 768
P = 128
TT = T // P
GROUPS, GH = 4, 4
STEPS = 12
CH = 512
PARTS = 6
MROW = PARTS * D
LEAD = 16
NST, NMX, NP = 2, 3, 2 * GH
Q_PART = (0, 0, 1, 0, 1, 2)
K_PART = (0, 1, 0, 2, 1, 0)
XS = 2048.0
QSCALE = 1.0 / 127.0
EPS = 1e-5
NEG = -3.0e38

BLOCKS = [(0, k) for k in range(4)] + [(1, k) for k in range(8)]


def width(n):
    qc, kb = BLOCKS[n]
    return (qc + 1) * CH - max(qc * CH, kb * P)


def is_diag(n):
    qc, kb = BLOCKS[n]
    return kb >= 4 * qc


def pieces(s):
    if s < 4:
        return [(j, s, 0, P * (s + 1), True) for j in range(GH)]
    t, sub = 4 + (s - 4) // 2, (s - 4) % 2
    out = []
    for j in (2 * sub, 2 * sub + 1):
        out += [(j, t, 0, CH, False), (j, t, CH, P * (t - 3), True)]
    return out


TASKS = {
    (0, 1): [("QK", 1, 0, 0)],
    (0, 2): [("QK", 1, 0, 1)],
    (0, 3): [("YT", 3, 1), ("QK", 1, 1, 0)],
    (0, 4): [("QK", 1, 1, 1)],
    (0, 5): [("UP", 0, 0)],
    (0, 7): [("FIN_T", 0)],
    (0, 8): [("UP", 0, 1)],
    (0, 9): [("FIN_T", 1), ("FIN_P", 0)],
    (0, 10): [("UP", 0, 2)],
    (0, 11): [("FIN_P", 1), ("FIN_T", 2)],
    (0, 12): [("FIN_O", 0), ("FIN_T", 3), ("YT", 0, 0)],
    (0, 14): [("UP", 0, 3)],
    (0, 15): [("FIN_O", 1), ("FIN_P", 2), ("FIN_O", 2)],
    (0, 16): [("FIN_P", 3)],
    (0, 18): [("V", 1, 0), ("FIN_O", 3), ("MT", 1)],
    (0, 19): [("UP", 0, 4)],
    (0, 20): [("UP", 0, 5)],
    (0, 21): [("LNS", 0), ("V", 1, 1)],
    (0, 22): [("DN", 0, 0)],
    (1, 0): [("DN", 0, 1)],
    (1, 1): [("UP", 1, 0), ("LNS", 1)],
    (1, 2): [("UP", 1, 1)],
    (1, 3): [("LNS", 2)],
    (1, 4): [("UP", 1, 2)],
    (1, 5): [("YT", 0, 1)],
    (1, 8): [("UP", 1, 3), ("LNS", 3)],
    (1, 9): [("UP", 1, 4), ("LNR",)],
    (1, 10): [("YT", 1, 0)],
    (1, 11): [("UP", 1, 5), ("LNA", 0)],
    (1, 13): [("LNA", 1)],
    (1, 14): [("LNA", 2), ("DN", 1, 0), ("LNA", 3)],
    (1, 15): [("DN", 1, 1)],
    (1, 16): [("MT", 2)],
    (1, 17): [("TX", 0, 0)],
    (1, 18): [("TX", 1, 0)],
    (1, 20): [("TX", 0, 1)],
    (1, 22): [("TX", 1, 1)],
    (2, 0): [("QK", 0, 0, 0)],
    (2, 1): [("QK", 0, 0, 1)],
    (2, 2): [("QK", 0, 1, 0)],
    (2, 3): [("QK", 0, 1, 1)],
    (2, 4): [("V", 0, 1)],
    (2, 5): [("YT", 1, 1)],
    (2, 7): [("V", 0, 0)],
    (2, 16): [("YT", 2, 0)],
    (2, 17): [("MT", 3)],
    (3, 8): [("YT", 2, 1)],
    (3, 12): [("YT", 3, 0)],
    (3, 17): [("MT", 0)],
}
HALVES = 2 * STEPS
PRO = ([("LNS", p) for p in range(4)] + [("LNR",)] + [("LNA", p) for p in range(4)]
       + [("TX", 0, 0), ("TX", 1, 0), ("TX", 0, 1), ("TX", 1, 1)]
       + [("QK", 0, 0, 0), ("QK", 0, 0, 1), ("QK", 0, 1, 0), ("QK", 0, 1, 1), ("V", 0, 0), ("V", 0, 1)]
       + [("MT", 0)])
EPI = ([("YT", 3, 1), ("FIN_T", 0), ("FIN_T", 1)]
       + [("FIN_P", 0), ("FIN_T", 2), ("FIN_P", 1), ("FIN_O", 0), ("FIN_T", 3), ("FIN_P", 2), ("FIN_O", 1)]
       + [("FIN_P", 3), ("FIN_O", 2), ("FIN_O", 3)])


def of_next(task):
    return task[0] in ("LNS", "LNR", "LNA", "TX") or task[:2] in (("QK", 0), ("V", 0)) or task == ("MT", 0)


def of_last(g, task):
    return task[0].startswith("FIN") or (g == 0 and task == ("YT", 3, 1))


def tasks_at(kind, g, h):
    return [t for t in TASKS.get((g, h), [])
            if not (kind == "first" and of_last(g, t)) and not (kind == "last" and of_next(t))]


LAG = {
    "scalar": {"TX": 0, "QK": 0, "UP": 0, "DN": 0, "FIN_T": 0, "MT": 1, "HI": 1},
    "vector": {"TX": 1, "QK": 1, "DN": 1, "FIN_O": 1, "LNS": 0, "LNR": 1, "LNA": 0, "V": 0, "UP": 0, "YT": 0, "FIN_P": 0},
    "gpsimd": {"QK": 1, "FIN_P": 0, "UP": 2},
    "sync": {"QK": 0, "MT": 0, "YT": 0, "FIN_O": 0},
}


def parts_at(engine, kind, g, h):
    lag = LAG[engine]
    found = []
    for late in range(max(lag.values()), -1, -1):
        at = HALVES * g + h - late
        if at >= 0:
            for t in tasks_at(kind, *divmod(at, HALVES)):
                if lag.get(t[0]) == late:
                    found.append(t)
                if t[0] == "UP" and lag.get("HI") == late:
                    found.append(("HI",) + t[1:])
    return found


def parts_of(engine, tasks):
    return [t for t in tasks if t[0] in LAG[engine]]


for _lags in LAG.values():
    for (_g, _h), _tasks in TASKS.items():
        for _t in _tasks:
            assert HALVES * _g + _h + max(_lags.get(_t[0], 0), _lags.get("HI", 0) * (_t[0] == "UP")) < HALVES * GROUPS

ORDER = {"pro": PRO, "epi": EPI}
for _kind in ("first", "mid", "last"):
    ORDER[_kind] = [t for g in range(GROUPS) for h in range(HALVES)
                    for t in tasks_at(_kind, g, h)]


class Tally:

    def __init__(self, events):
        self.seen = {k: [e for t in ORDER[k] for e in events(k, t)] for k in ORDER}
        n = {k: len(v) for k, v in self.seen.items()}
        self.base = {"pro": 0, "first": n["pro"], "mid": n["pro"] + n["first"]}
        self.each = n["mid"]
        self.base["last"] = self.base["mid"] + (B - 2) * self.each
        self.base["epi"] = self.base["last"] + n["last"]

    def at(self, kind, i, event):
        k = self.base[kind] + self.seen[kind].index(event) + 1
        return k + (i - 1) * self.each if kind == "mid" else k


def bank_uses():
    of = {}
    for kind in ("pro", "mid", "epi"):
        n = 0
        for t in ORDER[kind]:
            names = {"UP": ("gate", "up"), "LNS": (), "LNR": (), "LNA": (), "FIN_O": ()}.get(t[0], ("",))
            for name in names:
                of[kind, t, name] = n % 2
                n += 1
    for kind in ("first", "last"):
        of.update({(kind, t, name): b for (k, t, name), b in of.items() if k == "mid" and t in ORDER[kind]})
    return of


BANK = bank_uses()
HID_SCALE = 0.25 * QSCALE ** 2 / XS ** 2
FFN_SCALE = 2 * QSCALE
NEWTON = 3
LN_EACH = 2 * TT + 3 + 3 * NEWTON

USES = [Tally(lambda k, t, b=b: [(t, name) for name in ("", "gate", "up") if BANK.get((k, t, name)) == b])
        for b in range(2)]
BY = {name: Tally(lambda k, t, name=name: [t] if t[0] in name.split("+") else [])
      for name in ("TX", "QK", "UP+DN", "UP", "LNA", "YT", "FIN_P", "FIN_O", "MT")}


def tanh_before(kind, i, task):
    seen = BY["UP+DN"].seen[kind]
    k = seen.index(task) - 2
    if k >= 0:
        return kind, i, seen[k]
    return None if kind == "first" else ("mid", i - 1, seen[k])


def th_buffer(kind, task):
    return BY["UP+DN"].seen[kind].index(task) % 2


def ln_number(kind, i):
    return 0 if kind == "pro" else i + 1


def diag_count(i, g, n):
    return 2 * GH * (GROUPS * i + g) + (n if n < 4 else n - 4) + 1


def wait(eng, sem, count):
    if isinstance(count, int) and count <= 0:
        return
    eng.wait_ge(sem, count)


def stand(eng, sem):
    eng.sem_inc(sem, 1)


def build_program(nc, x, w_attn, b_attn, w_proj, b_proj, w_gate_t, w_up_t, w_down_t, rope_cos, rope_sin, out):
    fp32, bf16, fp16, i32 = mybir.dt.float32, mybir.dt.bfloat16, mybir.dt.float16, mybir.dt.int32
    ALU, ACT, AX = mybir.AluOpType, mybir.ActivationFunctionType, mybir.AxisListType

    parts_dram = nc.dram_tensor("parts_scratch", (2, 2, 3, P, T), bf16).ap()
    mrow_dram = nc.dram_tensor("maxima_scratch", (GROUPS, 3 * GH, T), bf16).ap()
    bias_dram = nc.dram_tensor("bias_scratch", (1, 2 * C), fp32).ap()
    x_tiles = x.rearrange("b (t p) c -> b p t c", p=P)
    out_tiles = out.rearrange("b (t p) c -> b p t c", p=P)

    with ExitStack() as ctx:
        def sb(name, shape, dt):
            return ctx.enter_context(nc.sbuf_tensor(name, shape, dt))

        def sem(name):
            return ctx.enter_context(nc.semaphore(name))

        w_qkv = sb("w_qkv", [P, 2, 3 * C], fp32)
        w_pr = sb("w_pr", [P, 2, C], fp32)
        w_ga = sb("w_ga", [P, 2, HID], bf16)
        w_up = sb("w_up", [P, 2, HID], bf16)
        w_dn = sb("w_dn", [P, HID // P, C], bf16)
        b_row = sb("b_row", [1, 2 * C], fp32)
        b_qk = sb("b_qk", [P, 4], fp32)
        b_v = sb("b_v", [P, C], fp32)
        b_pr = sb("b_pr", [P, C], fp32)
        ident = sb("ident", [P, P], fp32)
        ident16 = sb("ident16", [P, P], bf16)
        tri = sb("tri", [P, CH], bf16)
        parts = sb("parts", [P, 2, 3, T], bf16)
        xn = parts[:, :, :, :].rearrange("p a b t -> p (a b t)")[:, 0:2 * TT * C].bitcast(fp32)\
            .rearrange("p (t c) -> p t c", c=C)
        xnT = sb("xnT", [P, 2, T], fp32)
        xh = sb("xh", [P, 2, T], fp16)
        xl = sb("xl", [P, 2, T], fp16)
        qkf = sb("qkf", [P, 2, CH], fp32)
        qkr = sb("qkr", [P, 2, CH], fp32)
        q_st = sb("q_st", [P, GROUPS, GH, T], bf16)
        k_st = sb("k_st", [P, GROUPS, GH, T], bf16)
        v_pad = sb("v_pad", [P, TT, H, D + 1], fp32)
        pexp = sb("pexp", [P, NP, CH], fp32)
        yT = sb("yT", [P, 2, CH], fp32)
        yn = sb("yn", [P, TT, C], fp32)
        ynT = sb("ynT", [P, 2, 2, 2 * P], fp32)
        yrec = sb("yrec", [P, 2, 4 * GH], fp32)
        mx_a = sb("mx_a", [P, 2, GH, TT], fp32)
        mx_b = sb("mx_b", [P, 2, GH, TT // 2], fp32)
        mx_r = sb("mx_r", [P, GH, TT], fp32)
        mx_p = sb("mx_p", [P, TT, 3, GH], bf16)
        mT = sb("mT", [3 * GH, T], bf16)
        junk = sb("junk", [P, 2, CH], bf16)
        hT = sb("hT", [P, 2, HID // P, CH], fp16)
        th = sb("th", [P, 2, CH], fp32)
        gu = sb("gu", [P, 2, CH], fp32)
        g2 = sb("g2", [P, TT, C], fp32)
        cosb = g2[:, 0, :].rearrange("p (a n) -> p a n", a=2)
        sinb = g2[:, 1, :].rearrange("p (a n) -> p a n", a=2)
        xo = sb("xo", [P, 2, 2, C], fp32)
        so = sb("so", [P, 2, 2 * C], fp32)
        ln6 = sb("ln6", [P, TT, 6], fp32)
        lnv = sb("lnv", [P, TT, 2], fp32)
        lne = sb("lne", [P, TT], fp32)
        lnt = sb("lnt", [P, TT], fp32)
        rstd = sb("rstd", [P, TT], fp32)
        st = ctx.enter_context(nc.psum_tensor("st", [P, NST, CH], fp32))
        mx = ctx.enter_context(nc.psum_tensor("mx", [P, NMX, CH], fp32))
        acc = ctx.enter_context(nc.psum_tensor("acc", [P, CH], fp32))
        tb = ctx.enter_context(nc.psum_tensor("tb", [P, 2, CH], fp32))

        x_in = sem("x_in")
        w_in = {n: sem("w_in_" + n) for n in ("attn", "rope", "bias", "proj", "gate", "up", "down", "rest")}
        w_ready = sem("w_ready")
        w_chain = sem("w_chain")
        b_back = sem("b_back")
        const_ready = sem("const_ready")
        ones_ready = sem("ones_ready")
        ln_chain = sem("ln_chain")
        xn_ready = sem("xn_ready")
        xT_ready = sem("xT_ready")
        task_ready = [sem(f"task_ready{b}") for b in range(2)]
        task_free = [sem(f"task_free{b}") for b in range(2)]
        qk_first = sem("qk_first")
        qk_rest = sem("qk_rest")
        qk_second = sem("qk_second")
        qk_third = sem("qk_third")
        parts_out = sem("parts_out")
        stack_in = [sem(f"stack_in{g}") for g in range(GROUPS)]
        mx_ready = sem("mx_ready")
        mx_done = sem("mx_done")
        mp_chain = sem("mp_chain")
        mrow_out = sem("mrow_out")
        mrow_in = [sem(f"mrow_in{g}") for g in range(GROUPS)]
        st_ready = sem("st_ready")
        exp_done = sem("exp_done")
        tri_done = sem("tri_done")
        pv_done = sem("pv_done")
        acc_out = sem("acc_out")
        yrec_ready = sem("yrec_ready")
        const0 = sem("const0")
        h_high = sem("h_high")
        h_low = sem("h_low")
        th_ready = sem("th_ready")
        so_scaled = sem("so_scaled")
        xo_in = [sem(f"xo_in{b}") for b in range(2)]
        o_ready = sem("o_ready")
        o_out = [sem(f"o_out{b}") for b in range(2)]

        dve_stand, pool_stand, sp_stand = sem("dve_stand"), sem("pool_stand"), sem("sp_stand")

        block = ctx.enter_context(nc.Block())

        def bank(kind, task, name=""):
            return BANK[kind, task, name]

        def use(kind, i, task, name=""):
            return USES[bank(kind, task, name)].at(kind, i, (task, name))

        def wait_ready(eng, kind, i, task, name=""):
            eng.wait_ge(task_ready[bank(kind, task, name)], use(kind, i, task, name))

        def wait_done(eng, kind, i, task, name=""):
            eng.wait_ge(task_free[bank(kind, task, name)], use(kind, i, task, name))

        def last_of_previous(kind, i):
            return kind, i, ("YT", 3, 1)

        def run(engine, body, prologue, epilogue):
            prologue()
            body("first", 0)
            with engine.Fori(1, B - 1) as i:
                body("mid", i)
            body("last", B - 1)
            epilogue()

        def max_steps(kind, i, g, n):
            ahead = STEPS * g + n + LEAD
            du, s = divmod(ahead, STEPS)
            if kind == "last" and du >= GROUPS:
                return None
            return 4 * i + du, du % GROUPS, s

        w_raw = {
            "gate": hT[:, 0, :, :].rearrange("p m n -> p (m n)").bitcast(i32).rearrange("p (k n) -> p k n", k=2),
            "up": hT[:, 1, :, :].rearrange("p m n -> p (m n)").bitcast(i32).rearrange("p (k n) -> p k n", k=2),
            "down": yn[:, :, :].rearrange("p t c -> p (t c)")[:, 0:6 * C].bitcast(i32)
                .rearrange("p (k n) -> p k n", k=6),
        }

        @block.sync
        def _(sp):
            def load_stack(i, g, unit):
                hf = g // 2
                sp.wait_ge(parts_out, 32 * (2 * i + hf + 1))
                stand(sp, sp_stand)
                wait(sp, st_ready, STEPS * GH * (unit - GROUPS + 1))
                for stack, part_of, which in ((q_st, Q_PART, 0), (k_st, K_PART, 1)):
                    for s in range(PARTS):
                        src = parts_dram[hf, which, part_of[s], 64 * (g % 2):64 * (g % 2) + 64, :]
                        sp.dma_start(stack[D * s:D * s + D, g, :, :],
                                     src.rearrange("(j d) n -> d j n", d=D)).then_inc(stack_in[g], 16)

            def store_parts(kind, i, hf):
                for which in range(2):
                    sp.wait_ge(qk_third, BY["QK"].at(kind, i, ("QK", hf, which, 1)))
                    sp.dma_start(parts_dram[hf, which].rearrange("a p n -> p a n"),
                                 parts[:, which, :, :]).then_inc(parts_out, 16)

            def load_x(i):
                stand(sp, sp_stand)
                sp.dma_start(xn, batch(x_tiles, i)).then_inc(x_in, 16)

            def batch(tiles, i):
                if isinstance(i, int):
                    return tiles[i]
                return tiles[bass.ds(i, 1)].rearrange("b p t c -> p (b t) c")

            def store_maxima(kind, i, g):
                wait_done(sp, kind, i, ("MT", g))
                sp.dma_start(mrow_dram[g], mT[:, :]).then_inc(mrow_out, 16)
                sp.wait_ge(mrow_out, 16 * BY["MT"].at(kind, i, ("MT", g)))
                sp.dma_start(q_st[MROW:MROW + 3, g, :, :],
                             mrow_dram[g].rearrange("(a j) n -> a j n", a=3)).then_inc(mrow_in[g], 16)

            def load_xo(kind, i, tp):
                buf = tp % 2
                wait(sp, o_out[buf], 16 * (2 * i + tp // 2))
                stand(sp, sp_stand)
                sp.dma_start(xo[:, buf, :, :], batch(x_tiles, i)[:, 2 * tp:2 * tp + 2, :]).then_inc(xo_in[buf], 16)

            def store_out(kind, i, tp, done_of):
                buf = tp % 2
                sp.wait_ge(o_ready, BY["FIN_O"].at(kind, i, ("FIN_O", tp)))
                stand(sp, sp_stand)
                sp.dma_start(batch(out_tiles, done_of)[:, 2 * tp:2 * tp + 2, :], xo[:, buf, :, :])\
                    .then_inc(o_out[buf], 16)

            def task(kind, i, g, t):
                if t == ("QK", 1, 1, 1):
                    store_parts(kind, i, 1)
                    load_stack(i, 2, 4 * i + 2)
                    load_stack(i, 3, 4 * i + 3)
                    if kind != "last":
                        load_x(i + 1)
                if t == ("QK", 0, 1, 1):
                    store_parts(kind, i, 0)
                    load_stack(i + 1, 0, 4 * i + 4)
                    load_stack(i + 1, 1, 4 * i + 5)
                if t[0] == "MT":
                    store_maxima(kind, i, t[1])
                if t == ("YT", 2, 1):
                    load_xo(kind, i, 0)
                    load_xo(kind, i, 1)
                if t[0] == "FIN_O":
                    store_out(kind, i, t[1], i - 1)
                    if t[1] < 2:
                        load_xo(kind, i - 1, t[1] + 2)

            def prologue():
                load_x(0)
                sp.dma_start(w_qkv[:, :, :], w_attn.rearrange("(k p) n -> p k n", p=P)).then_inc(w_in["attn"], 16)
                sp.dma_start(cosb, rope_cos.rearrange("p (a n) -> p a n", a=2)).then_inc(w_in["rope"], 16)
                sp.dma_start(sinb, rope_sin.rearrange("p (a n) -> p a n", a=2)).then_inc(w_in["rope"], 16)
                sp.dma_start(b_row[:, :], b_attn[:, 0:2 * C]).then_inc(w_in["bias"], 16)
                sp.wait_ge(w_ready, 2)
                sp.dma_start(bias_dram, b_row[:, :]).then_inc(b_back, 16)
                sp.wait_ge(b_back, 16)
                sp.dma_start(b_qk[:, :], bias_dram.rearrange("o (t p) -> p (o t)", p=P),
                             allow_slow_non_contiguous=True).then_inc(b_back, 16)
                sp.dma_start(b_v[:, :], b_attn[:, 2 * C:3 * C].broadcast_to([P, C])).then_inc(w_in["rest"], 16)
                sp.dma_start(b_pr[:, :], b_proj.broadcast_to([P, C])).then_inc(w_in["rest"], 16)
                sp.dma_start(w_pr[:, :, :], w_proj.rearrange("(k p) n -> p k n", p=P)).then_inc(w_in["proj"], 16)
                sp.dma_start(w_raw["gate"], w_gate_t.rearrange("(k p) n -> p k n", p=P)).then_inc(w_in["gate"], 16)
                sp.dma_start(w_raw["up"], w_up_t.rearrange("(k p) n -> p k n", p=P)).then_inc(w_in["up"], 16)
                sp.dma_start(w_raw["down"], w_down_t.rearrange("(k p) n -> p k n", p=P)).then_inc(w_in["down"], 16)
                store_parts("pro", 0, 0)
                load_stack(0, 0, 0)
                load_stack(0, 1, 1)
                store_maxima("pro", 0, 0)

            def body(kind, i):
                for g in range(GROUPS):
                    for h in range(HALVES):
                        for t in parts_at("sync", kind, g, h):
                            task(kind, i, g, t)

            def epilogue():
                for t in parts_of("sync", EPI):
                    task("epi", B, 0, t)
                for buf in range(2):
                    sp.wait_ge(o_out[buf], 16 * 2 * B)

            run(sp, body, prologue, epilogue)

        @block.tensor
        def _(pe):
            def take(kind, i, task, name=""):
                b = bank(kind, task, name)
                wait(pe, task_free[b], use(kind, i, task, name) - 1)
                return tb[:, b, :], task_ready[b]

            def scores(i, g, n, j):
                qc, kb = BLOCKS[n]
                w = width(n)
                index = STEPS * GH * (4 * i + g) + GH * n + j
                wait(pe, exp_done, index - NST + 1)
                if n == 0 and j == 0:
                    pe.wait_ge(mrow_in[g], 16 * (i + 1))
                q0 = (qc + 1) * CH - w
                nc.tensor.matmul(st[:, (GH * n + j) % NST, 0:w], k_st[0:MROW + 3, g, j, kb * P:(kb + 1) * P],
                                 q_st[0:MROW + 3, g, j, q0:q0 + w], start=True, stop=True).then_inc(st_ready, 1)

            def max_piece(unit, g, s, c, i_next):
                j, t, k0, w, _ = pieces(s)[c]
                if s == 0 and c == 0:
                    pe.wait_ge(stack_in[g], 16 * 2 * PARTS * (i_next + 1))
                index = (STEPS * unit + s) * GH + c
                wait(pe, mx_done, index - NMX + 1)
                nc.tensor.matmul(mx[:, (GH * s + c) % NMX, 0:w], q_st[0:MROW, g, j, t * P:(t + 1) * P],
                                 k_st[0:MROW, g, j, k0:k0 + w], start=True, stop=True).then_inc(mx_ready, 1)

            def values(i, g, n):
                qc, kb = BLOCKS[n]
                w = width(n)
                if is_diag(n):
                    pe.wait_ge(tri_done, diag_count(i, g, n))
                else:
                    pe.wait_ge(exp_done, GH * (STEPS * (4 * i + g) + n + 1))
                if kb == 0:
                    wait(pe, acc_out, 2 * (4 * i + g) + qc)
                for j in range(GH):
                    mm = nc.tensor.matmul(acc[32 * j:32 * j + D + 1, CH - w:CH], v_pad[:, kb, GH * g + j, :],
                                          pexp[:, GH * (n % 2) + j, 0:w],
                                          start=kb == 0, stop=kb == 4 * qc + 3)
                mm.then_inc(pv_done, 1)

            def task(kind, i, g, t):
                if t[0] == "TX":
                    _, kt, c = t
                    pe.wait_ge(xn_ready, BY["LNA"].at(kind, i, ("LNA", 2 * c + 1)))
                    dst, ready = take(kind, i, t)
                    for tt in range(4):
                        mm = nc.tensor.transpose(dst[:, tt * P:(tt + 1) * P],
                                                 xn[:, 4 * c + tt, kt * P:(kt + 1) * P], ident[:, :])
                    mm.then_inc(ready, 1)
                if t[0] == "QK":
                    _, hf, which, c = t
                    if hf == 0 and which == 0 and c == 0:
                        pe.wait_ge(xT_ready, BY["TX"].at(kind, i, ("TX", 1, 1)))
                    dst, ready = take(kind, i, t)
                    col = which * C + hf * P
                    for kt in range(2):
                        mm = nc.tensor.matmul(dst, w_qkv[:, kt, col:col + P], xnT[:, kt, c * CH:(c + 1) * CH],
                                              start=kt == 0, stop=kt == 1)
                    mm.then_inc(ready, 1)
                if t[0] == "V":
                    _, hf, tq = t
                    dst, ready = take(kind, i, t)
                    for tt in range(4):
                        for kt in range(2):
                            mm = nc.tensor.matmul(dst[:, tt * P:(tt + 1) * P],
                                                  xnT[:, kt, (4 * tq + tt) * P:(4 * tq + tt + 1) * P],
                                                  w_qkv[:, kt, 2 * C + hf * P:2 * C + hf * P + P],
                                                  start=kt == 0, stop=kt == 1)
                    mm.then_inc(ready, 1)
                if t[0] == "UP":
                    _, c, m = t
                    for name, w in (("gate", w_ga), ("up", w_up)):
                        dst, ready = take(kind, i, t, name)
                        for kt in range(2):
                            for xpart in (xh, xl):
                                mm = nc.tensor.matmul(dst, w[:, kt, m * P:(m + 1) * P],
                                                      xpart[:, kt, c * CH:(c + 1) * CH],
                                                      start=kt == 0 and xpart is xh, stop=kt == 1 and xpart is xl)
                        mm.then_inc(ready, 1)
                if t[0] == "DN":
                    _, c, tp = t
                    if tp == 0:
                        pe.wait_ge(h_low, BY["UP"].at(kind, i, ("UP", c, HID // P - 1)))
                    dst, ready = take(kind, i, t)
                    for t2 in range(2):
                        for m in range(HID // P):
                            for low in range(2):
                                mm = nc.tensor.matmul(dst[:, t2 * C:(t2 + 1) * C],
                                                      hT[:, low, m, (2 * tp + t2) * P:(2 * tp + t2 + 1) * P],
                                                      w_dn[:, m, :], start=m == 0 and not low,
                                                      stop=m == HID // P - 1 and low == 1)
                    mm.then_inc(ready, 1)
                if t[0] == "YT":
                    _, yg, qc = t
                    unit_i = i - 1 if (yg, qc) == (3, 1) else i
                    pe.wait_ge(acc_out, 2 * (4 * unit_i + yg) + qc + 1)
                    dst, ready = take(kind, i, t)
                    for tt in range(4):
                        mm = nc.tensor.transpose(dst[:, tt * P:(tt + 1) * P], yT[:, qc, tt * P:(tt + 1) * P],
                                                 ident[:, :])
                    mm.then_inc(ready, 1)
                if t[0] == "FIN_T":
                    _, tp = t
                    if tp == 0:
                        wait_done(pe, kind, i, ("YT", 3, 1))
                    dst, ready = take(kind, i, t)
                    for kt in range(2):
                        for t2 in range(2):
                            mm = nc.tensor.transpose(dst[:, kt * 2 * P + t2 * P:kt * 2 * P + (t2 + 1) * P],
                                                     yn[:, 2 * tp + t2, kt * P:(kt + 1) * P], ident[:, :])
                    mm.then_inc(ready, 1)
                if t[0] == "FIN_P":
                    _, tp = t
                    wait_done(pe, kind, i, ("FIN_T", tp))
                    dst, ready = take(kind, i, t)
                    for t2 in range(2):
                        for kt in range(2):
                            mm = nc.tensor.matmul(dst[:, t2 * C:(t2 + 1) * C],
                                                  ynT[:, tp % 2, kt, t2 * P:(t2 + 1) * P], w_pr[:, kt, :],
                                                  start=kt == 0, stop=kt == 1)
                    mm.then_inc(ready, 1)
                if t[0] == "MT":
                    pe.wait_ge(mp_chain, 5 * BY["MT"].at(kind, i, t))
                    dst, ready = take(kind, i, t)
                    for tt in range(TT):
                        mm = nc.tensor.transpose(dst[0:3 * GH, :].bitcast(bf16)[:, tt * P:(tt + 1) * P],
                                                 mx_p[:, tt, :, :].rearrange("p a j -> p (a j)"), ident16[:, :])
                    mm.then_inc(ready, 1)

            def prologue():
                pe.wait_ge(const_ready, 3)
                for t in PRO[:-1]:
                    if t == ("QK", 0, 0, 0):
                        pe.wait_ge(w_ready, 1)
                    task("pro", 0, 0, t)
                for ahead in range(LEAD):
                    unit, s = divmod(ahead, STEPS)
                    for c in range(GH):
                        max_piece(unit, unit, s, c, 0)
                    if ahead == STEPS:
                        task("pro", 0, 0, ("MT", 0))
                pe.wait_ge(w_ready, 5)
                pe.wait_ge(w_in["proj"], 16)
                for tq in range(2):
                    wait_done(pe, "pro", 0, ("V", 0, tq))

            def body(kind, i):
                for g in range(GROUPS):
                    for n in range(STEPS):
                        ahead = max_steps(kind, i, g, n)
                        i_next = i + (STEPS * g + n + LEAD) // (STEPS * GROUPS)
                        if ahead:
                            unit, mg, s = ahead
                        for half in range(2):
                            scores(i, g, n, 2 * half)
                            if ahead:
                                max_piece(unit, mg, s, 2 * half, i_next)
                            scores(i, g, n, 2 * half + 1)
                            if half == 1:
                                if (g, n) != (0, 0):
                                    values(i, *divmod(STEPS * g + n - 1, STEPS))
                                elif kind != "first":
                                    values(i - 1, GROUPS - 1, STEPS - 1)
                            if ahead:
                                max_piece(unit, mg, s, 2 * half + 1, i_next)
                            for t in tasks_at(kind, g, 2 * n + half):
                                task(kind, i, g, t)

            def epilogue():
                values(B - 1, GROUPS - 1, STEPS - 1)
                for t in EPI:
                    task("epi", B, 0, t)

            run(pe, body, prologue, epilogue)

        @block.scalar
        def _(act):
            def exps(i, g, n, heads):
                w = width(n)
                for j in heads:
                    index = STEPS * GH * (4 * i + g) + GH * n + j
                    if j == 0:
                        wait(act, pv_done, STEPS * (4 * i + g) + n - 1)
                    act.wait_ge(st_ready, index + 1)
                    nc.scalar.activation(pexp[:, GH * (n % 2) + j, 0:w], st[:, (GH * n + j) % NST, 0:w], ACT.Exp,
                                         scale=1.0 / np.sqrt(D)).then_inc(exp_done, 1)

            def copy_acc(i, g, qc):
                act.wait_ge(pv_done, STEPS * (4 * i + g) + (4 if qc == 0 else STEPS))
                nc.scalar.activation(yT[:, qc, :], acc[:, :], ACT.Copy).then_inc(acc_out, 1)

            def task(kind, i, g, t):
                if t[0] == "TX":
                    _, kt, c = t
                    wait_ready(act, kind, i, t)
                    src = tb[:, bank(kind, t), :]
                    nc.scalar.activation(xnT[:, kt, c * CH:(c + 1) * CH], src, ACT.Copy)
                    nc.scalar.activation(xh[:, kt, c * CH:(c + 1) * CH], src, ACT.Copy, scale=XS)\
                        .then_inc(xT_ready, 1)
                if t[0] == "QK":
                    _, hf, which, c = t
                    k = BY["QK"].at(kind, i, t)
                    src = tb[:, bank(kind, t), :]
                    bias = b_qk[:, 2 * which + hf:2 * which + hf + 1]
                    wait_ready(act, kind, i, t)
                    wait(act, qk_rest, k - 2)
                    nc.scalar.activation(qkf[:, c, :], src, ACT.Identity, bias=bias)
                    if kind != "pro":
                        act.wait_ge(parts_out, 32 * (2 * i + 2 - hf))
                    nc.scalar.activation(parts[:, which, 0, c * CH:(c + 1) * CH], src, ACT.Identity, bias=bias)\
                        .then_inc(task_free[bank(kind, t)], 1)
                if t[0] == "UP":
                    _, c, m = t
                    wait_ready(act, kind, i, t, "gate")
                    wait_th(kind, i, t)
                    nc.scalar.activation(th[:, th_buffer(kind, t), :], tb[:, bank(kind, t, "gate"), :],
                                         ACT.Tanh, scale=0.5 * QSCALE / XS).then_inc(th_ready, 1)
                if t[0] == "HI":
                    _, c, m = t
                    wait_done(act, kind, i, ("UP", c, m), "up")
                    nc.scalar.activation(hT[:, 0, m, :], gu[:, m % 2, :], ACT.Copy).then_inc(h_high, 1)
                if t[0] == "DN":
                    wait_ready(act, kind, i, t)
                    wait_th(kind, i, t)
                    nc.scalar.activation(th[:, th_buffer(kind, t), :], tb[:, bank(kind, t), :],
                                         ACT.Tanh, scale=0.5 * FFN_SCALE).then_inc(th_ready, 1)
                if t[0] == "FIN_T":
                    _, tp = t
                    wait_ready(act, kind, i, t)
                    b = bank(kind, t)
                    nc.scalar.activation(ynT[:, tp % 2, :, :], tb[:, b, :].rearrange("p (k n) -> p k n", k=2),
                                         ACT.Copy).then_inc(task_free[b], 1)
                if t[0] == "MT":
                    k = BY["MT"].at(kind, i, t)
                    b = bank(kind, t)
                    wait_ready(act, kind, i, t)
                    wait(act, mrow_out, 16 * (k - 1))
                    nc.scalar.activation(mT[:, :], tb[0:3 * GH, b, :].bitcast(bf16), ACT.Copy)\
                        .then_inc(task_free[b], 1)

            def wait_th(kind, i, t):
                before = tanh_before(kind, i, t)
                if before:
                    wait_done(act, *before, "gate" if before[2][0] == "UP" else "")

            def prologue():
                act.wait_ge(b_back, 32)
                for t in parts_of("scalar", PRO):
                    task("pro", 0, 0, t)

            def body(kind, i):
                for g in range(GROUPS):
                    for n in range(STEPS):
                        for half in range(2):
                            exps(i, g, n, (2 * half, 2 * half + 1))
                            for t in parts_at("scalar", kind, g, 2 * n + half):
                                task(kind, i, g, t)
                        if n == 0 and (g > 0 or kind != "first"):
                            copy_acc(i if g else i - 1, (g - 1) % GROUPS, 1)
                        if n == 4:
                            copy_acc(i, g, 0)

            def epilogue():
                copy_acc(B - 1, GROUPS - 1, 1)
                for t in parts_of("scalar", EPI):
                    task("epi", B, 0, t)

            run(act, body, prologue, epilogue)

        @block.vector
        def _(dve):
            def max_take(unit, g, s, which=range(GH)):
                par = g % 2
                for c in which:
                    j, t, k0, w, diag = pieces(s)[c]
                    index = (STEPS * unit + s) * GH + c
                    dve.wait_ge(mx_ready, index + 1)
                    dst = mx_b[:, par, j, t - 4:t - 3] if k0 else mx_a[:, par, j, t:t + 1]
                    src = mx[:, (GH * s + c) % NMX, 0:w]
                    if diag:
                        wait(dve, mx_done, index - 1)
                        stand(dve, dve_stand)
                        nc.vector.tensor_tensor_reduce(out=junk[:, c % 2, 0:w], in0=src, in1=tri[:, CH - w:CH],
                                                       scale=1.0, scalar=NEG, op0=ALU.add, op1=ALU.max,
                                                       accum_out=dst).then_inc(mx_done, 1)
                    else:
                        nc.vector.reduce_max(dst, src, AX.X).then_inc(mx_done, 1)

            def mp_step(ins, count):
                ins.then_inc(mp_chain, 1)
                dve.wait_ge(mp_chain, count)

            def split_maxima(kind, i, t, unit):
                par = t[1] % 2
                base = 5 * (BY["MT"].at(kind, i, t) - 1)
                m = mx_a[:, par, :, :]
                m_t = mx_a[:, par, :, :].rearrange("p j t -> p t j")
                r_t = mx_r[:, :, :].rearrange("p j t -> p t j")
                dve.wait_ge(mx_done, STEPS * GH * (unit + 1))
                mp_step(nc.vector.tensor_tensor(m[:, :, 4:8], m[:, :, 4:8], mx_b[:, par, :, :], ALU.max), base + 1)
                wait(dve, mrow_out, 16 * (BY["MT"].at(kind, i, t) - 1))
                mp_step(nc.vector.tensor_scalar(mx_p[:, :, 0, :], m_t, -1.0, None, ALU.mult), base + 2)
                mp_step(nc.vector.scalar_tensor_tensor(out=r_t, in0=m_t, scalar=-1.0, in1=mx_p[:, :, 0, :],
                                                       op0=ALU.mult, op1=ALU.subtract), base + 3)
                mp_step(nc.vector.tensor_copy(mx_p[:, :, 1, :], r_t), base + 4)
                nc.vector.tensor_tensor(mx_p[:, :, 2, :], r_t, mx_p[:, :, 1, :], ALU.subtract).then_inc(mp_chain, 1)

            def ln_step(ins, kind, i, k):
                ins.then_inc(ln_chain, 1)
                dve.wait_ge(ln_chain, LN_EACH * ln_number(kind, i) + k)

            def task(kind, i, g, t):
                if t[0] == "LNS":
                    _, p = t
                    if p == 0:
                        dve.wait_ge(x_in, 16 * (ln_number(kind, i) + 1))
                    for e in range(2):
                        tt = 2 * p + e
                        ln_step(nc.vector.bn_stats(ln6[:, tt, :], xn[:, tt, :]), kind, i, 2 * tt + 1)
                        stand(dve, dve_stand)
                        ln_step(nc.vector.bn_aggr(lnv[:, tt, :], ln6[:, tt, :]), kind, i, 2 * tt + 2)
                if t[0] == "LNR":
                    k = 2 * TT
                    ln_step(nc.vector.tensor_scalar(lne[:, :], lnv[:, :, 1], EPS, None, ALU.add), kind, i, k + 1)
                    ln_step(nc.vector.tensor_scalar(rstd[:, :].bitcast(i32), lne[:, :].bitcast(i32), 1, None,
                                                    ALU.arith_shift_right), kind, i, k + 2)
                    ln_step(nc.vector.tensor_scalar(rstd[:, :].bitcast(i32), rstd[:, :].bitcast(i32), -1.0,
                                                    float(0x5F3759DF), ALU.mult, ALU.add), kind, i, k + 3)
                    for it in range(NEWTON):
                        k = 2 * TT + 3 + 3 * it
                        ln_step(nc.vector.tensor_tensor(lnt[:, :], rstd[:, :], rstd[:, :], ALU.mult), kind, i, k + 1)
                        ln_step(nc.vector.scalar_tensor_tensor(out=lnt[:, :], in0=lnt[:, :], scalar=-0.5,
                                                               in1=lne[:, :], op0=ALU.mult, op1=ALU.mult),
                                kind, i, k + 2)
                        ln_step(nc.vector.scalar_tensor_tensor(out=rstd[:, :], in0=lnt[:, :], scalar=1.5,
                                                               in1=rstd[:, :], op0=ALU.add, op1=ALU.mult),
                                kind, i, k + 3)
                if t[0] == "LNA":
                    _, p = t
                    for e in range(2):
                        tt = 2 * p + e
                        ins = nc.vector.tensor_scalar(xn[:, tt, :], xn[:, tt, :], lnv[:, tt, 0:1], rstd[:, tt:tt + 1],
                                                      ALU.subtract, ALU.mult)
                    ins.then_inc(xn_ready, 1)
                if t[0] == "TX":
                    _, kt, c = t
                    b = bank(kind, t)
                    dve.wait_ge(xT_ready, BY["TX"].at(kind, i, t))
                    nc.vector.scalar_tensor_tensor(out=xl[:, kt, c * CH:(c + 1) * CH], in0=tb[:, b, :], scalar=XS,
                                                   in1=xh[:, kt, c * CH:(c + 1) * CH], op0=ALU.mult,
                                                   op1=ALU.subtract).then_inc(task_free[b], 1)
                if t[0] == "QK":
                    _, hf, which, c = t
                    k = BY["QK"].at(kind, i, t)
                    wait_done(dve, kind, i, t)
                    wait(dve, qk_third, k - 2)
                    part = parts[:, which, :, c * CH:(c + 1) * CH]
                    nc.vector.tensor_tensor(qkr[:, c, :], qkf[:, c, :], part[:, 0, :], ALU.subtract)\
                        .then_inc(qk_rest, 1)
                    dve.wait_ge(qk_rest, k)
                    nc.vector.tensor_copy(part[:, 1, :], qkr[:, c, :]).then_inc(qk_second, 1)
                if t[0] == "V":
                    _, hf, tq = t
                    b = bank(kind, t)
                    wait_ready(dve, kind, i, t)
                    nc.vector.tensor_tensor(
                        v_pad[:, 4 * tq:4 * tq + 4, 8 * hf:8 * hf + 8, 0:D],
                        tb[:, b, :].rearrange("p (t h d) -> p t h d", t=4, d=D),
                        b_v[:, hf * P:(hf + 1) * P].rearrange("p (o h d) -> p o h d", o=1, d=D)
                        .broadcast_to([P, 4, 8, D]), ALU.add).then_inc(task_free[b], 1)
                if t[0] == "UP":
                    _, c, m = t
                    k = BY["UP+DN"].at(kind, i, t)
                    ba, bb = bank(kind, t, "gate"), bank(kind, t, "up")
                    dve.wait_ge(th_ready, k)
                    wait(dve, h_low, BY["UP"].at(kind, i, t) - 2)
                    h = gu[:, m % 2, :]
                    nc.vector.scalar_tensor_tensor(out=h, in0=th[:, th_buffer(kind, t), :], scalar=1.0,
                                                   in1=tb[:, ba, :], op0=ALU.add, op1=ALU.mult)\
                        .then_inc(task_free[ba], 1)
                    wait_done(dve, kind, i, t, "gate")
                    wait_ready(dve, kind, i, t, "up")
                    nc.vector.scalar_tensor_tensor(out=h, in0=h, scalar=HID_SCALE, in1=tb[:, bb, :],
                                                   op0=ALU.mult, op1=ALU.mult).then_inc(task_free[bb], 1)
                if t[0] == "DN":
                    _, c, tp = t
                    b = bank(kind, t)
                    k = BY["UP+DN"].at(kind, i, t)
                    dve.wait_ge(th_ready, k)
                    if kind != "first" and (c, tp) == (0, 0):
                        dve.wait_ge(so_scaled, BY["FIN_P"].at(kind, i, ("FIN_P", 3)))
                    nc.vector.scalar_tensor_tensor(
                        out=g2[:, 4 * c + 2 * tp:4 * c + 2 * tp + 2, :].rearrange("p t c -> p (t c)"),
                        in0=th[:, th_buffer(kind, t), :], scalar=1.0, in1=tb[:, b, :],
                        op0=ALU.add, op1=ALU.mult).then_inc(task_free[b], 1)
                if t[0] == "YT":
                    _, yg, qc = t
                    b = bank(kind, t)
                    k = BY["YT"].at(kind, i, t)
                    wait_ready(dve, kind, i, t)
                    y4 = tb[:, b, :].rearrange("p (t j r) -> p t j r", t=4, r=32)
                    nc.vector.reciprocal(yrec[:, qc, :].rearrange("p (t j o) -> p t j o", t=4, o=1),
                                         y4[:, :, :, D:D + 1]).then_inc(yrec_ready, 1)
                    dve.wait_ge(yrec_ready, k)
                    nc.vector.tensor_tensor(
                        yn[:, 4 * qc:4 * qc + 4, yg * 64:yg * 64 + 64].rearrange("p t (j d) -> p t j d", d=D),
                        y4[:, :, :, 0:D],
                        yrec[:, qc, :].rearrange("p (t j o) -> p t j o", t=4, o=1).broadcast_to([P, 4, GH, D]),
                        ALU.mult).then_inc(task_free[b], 1)
                if t[0] == "FIN_P":
                    _, tp = t
                    b = bank(kind, t)
                    k = BY["FIN_P"].at(kind, i, t)
                    wait_ready(dve, kind, i, t)
                    if tp >= 2:
                        dve.wait_ge(o_ready, k - 2)
                    nc.vector.tensor_tensor(so[:, tp % 2, :].rearrange("p (t c) -> p t c", t=2),
                                            tb[:, b, :].rearrange("p (t c) -> p t c", t=2),
                                            b_pr[:, :].rearrange("p (o c) -> p o c", o=1).broadcast_to([P, 2, C]),
                                            ALU.add).then_inc(task_free[b], 1)
                if t[0] == "FIN_O":
                    _, tp = t
                    k = BY["FIN_O"].at(kind, i, t)
                    dve.wait_ge(so_scaled, k)
                    dve.wait_ge(xo_in[tp % 2], 16 * (2 * (i - 1) + tp // 2 + 1))
                    o = xo[:, tp % 2, :, :].rearrange("p t c -> p (t c)")
                    nc.vector.scalar_tensor_tensor(out=o, in0=so[:, tp % 2, :], scalar=0.5 * FFN_SCALE, in1=o,
                                                   op0=ALU.mult, op1=ALU.add).then_inc(o_ready, 1)

            def turn(we, wo, cos, sin, tmp, count):
                for dst, a, b in ((tmp[0], we, cos), (tmp[1], wo, sin), (tmp[2], wo, cos), (tmp[3], we, sin)):
                    last = nc.vector.tensor_tensor(dst, a, b, ALU.mult)
                last.then_inc(w_chain, 1)
                dve.wait_ge(w_chain, count)
                nc.vector.tensor_tensor(we, tmp[0], tmp[1], ALU.subtract)
                return nc.vector.tensor_tensor(wo, tmp[2], tmp[3], ALU.add)

            def prologue():
                nc.vector.memset(acc[:, :], 0.0)
                for t in PRO[:9]:
                    task("pro", 0, 0, t)
                dve.wait_ge(w_in["rope"], 32)
                dve.wait_ge(w_in["attn"], 16)
                wv = w_qkv[:, :, 0:2 * C].rearrange("p k (n two) -> p k n two", two=2)
                cos, sin = (g2[:, k:k + 1, :] for k in range(2))
                tmp = [pexp[:, k, :].rearrange("p (k n) -> p k n", k=2) for k in range(4)]
                turn(wv[:, :, :, 0], wv[:, :, :, 1], cos.broadcast_to([P, 2, C]), sin.broadcast_to([P, 2, C]),
                     tmp, 1).then_inc(w_ready, 1)
                dve.wait_ge(w_in["bias"], 16)
                bv = b_row[:, :].rearrange("p (n two) -> p n two", two=2)
                tmp = [pexp[0:1, 4 + k, 0:C] for k in range(4)]
                turn(bv[:, :, 0], bv[:, :, 1], cos[0:1, 0, :], sin[0:1, 0, :], tmp, 2).then_inc(w_ready, 1)
                for t in PRO[9:-1]:
                    if t[0] == "V" and t[2] == 0:
                        dve.wait_ge(w_in["rest"], 32)
                        dve.wait_ge(ones_ready, 2)
                    task("pro", 0, 0, t)
                dve.wait_ge(w_in["gate"], 16)
                nc.vector.tensor_copy(w_ga[:, :, :], w_raw["gate"]).then_inc(w_ready, 1)
                dve.wait_ge(w_in["up"], 16)
                nc.vector.tensor_copy(w_up[:, :, :], w_raw["up"]).then_inc(w_ready, 1)
                dve.wait_ge(w_in["down"], 16)
                nc.vector.tensor_copy(w_dn[:, :, :], w_raw["down"]).then_inc(w_ready, 1)
                dve.wait_ge(const_ready, 4)
                for ahead in range(LEAD):
                    unit, s = divmod(ahead, STEPS)
                    if ahead == STEPS:
                        split_maxima("pro", 0, ("MT", 0), 0)
                    max_take(unit, unit, s)
                dve.wait_ge(w_ready, 5)

            def body(kind, i):
                for g in range(GROUPS):
                    for n in range(STEPS):
                        ahead = max_steps(kind, i, g, n)
                        for half in range(2):
                            for t in tasks_at(kind, g, 2 * n + half):
                                if t[0] == "MT":
                                    split_maxima(kind, i, t, 4 * i + g + 1)
                            if ahead:
                                max_take(*ahead, (2 * half, 2 * half + 1))
                            for t in parts_at("vector", kind, g, 2 * n + half):
                                task(kind, i, g, t)

            def epilogue():
                for t in EPI:
                    task("epi", B, 0, t)

            run(dve, body, prologue, epilogue)

        @block.gpsimd
        def _(pool):
            def mask(i, g, n):
                pool.wait_ge(exp_done, GH * (STEPS * (4 * i + g) + n + 1))
                stand(pool, pool_stand)
                t = pexp[:, GH * (n % 2):GH * (n % 2) + GH, 0:P]
                nc.gpsimd.affine_select(out=t, in_=t, compare_op=ALU.is_ge, fill=0.0, base=0,
                                        pattern=[[0, GH], [1, P]], channel_multiplier=-1).then_inc(tri_done, 1)

            def task(kind, i, g, t):
                if t[0] == "QK":
                    _, hf, which, c = t
                    pool.wait_ge(qk_second, BY["QK"].at(kind, i, t))
                    part = parts[:, which, :, c * CH:(c + 1) * CH]
                    nc.gpsimd.tensor_tensor(part[:, 2, :], qkr[:, c, :], part[:, 1, :], ALU.subtract)\
                        .then_inc(qk_third, 1)
                if t[0] == "UP":
                    _, c, m = t
                    pool.wait_ge(h_high, BY["UP"].at(kind, i, t))
                    nc.gpsimd.tensor_tensor(hT[:, 1, m, :], gu[:, m % 2, :], hT[:, 0, m, :], ALU.subtract)\
                        .then_inc(h_low, 1)
                if t[0] == "FIN_P":
                    _, tp = t
                    wait_done(pool, kind, i, t)
                    s = so[:, tp % 2, :]
                    nc.gpsimd.tensor_tensor(s, s, g2[:, 2 * tp:2 * tp + 2, :].rearrange("p t c -> p (t c)"),
                                            ALU.mult).then_inc(so_scaled, 1)

            def prologue():
                pool.memset(ident[:, :], 0.0).then_inc(const0, 1)
                pool.memset(ident16[:, :], 0.0).then_inc(const0, 1)
                pool.memset(tri[:, :], 0.0).then_inc(const0, 1)
                pool.wait_ge(const0, 3)
                for m in (ident, ident16):
                    pool.affine_select(out=m[:, :], in_=m[:, :], compare_op=ALU.not_equal, fill=1.0, base=0,
                                       pattern=[[-1, P]], channel_multiplier=1).then_inc(const_ready, 1)
                pool.wait_ge(const_ready, 2)
                pool.memset(k_st[MROW:MROW + 3, :, :, :].rearrange("p g j n -> p (g j n)").bitcast(fp32),
                            float(np.uint32(0x3F803F80).view(np.float32))).then_inc(const_ready, 1)
                pool.wait_ge(const_ready, 3)
                pool.affine_select(out=tri[:, CH - P:CH], in_=tri[:, CH - P:CH], compare_op=ALU.is_ge, fill=NEG,
                                   base=0, pattern=[[-1, P]], channel_multiplier=1).then_inc(const_ready, 1)
                pool.memset(v_pad[:, :, 0:8, D:D + 1], 1.0).then_inc(ones_ready, 1)
                pool.memset(v_pad[:, :, 8:16, D:D + 1], 1.0).then_inc(ones_ready, 1)
                for t in parts_of("gpsimd", PRO):
                    task("pro", 0, 0, t)

            def body(kind, i):
                for g in range(GROUPS):
                    for n in range(STEPS):
                        for half in range(2):
                            for t in parts_at("gpsimd", kind, g, 2 * n + half):
                                task(kind, i, g, t)
                        if is_diag(n):
                            mask(i, g, n)

            def epilogue():
                for t in parts_of("gpsimd", EPI):
                    task("epi", B, 0, t)

            run(pool, body, prologue, epilogue)


_OUT = ((B, T, C), "float32")


def kernel(**inputs):
    import concourse.bacc as _bacc
    from concourse import mybir as _mybir
    from concourse.bass_utils import run_bass_kernel_spmd as _run

    theta = 1.0 / np.power(np.float32(10000.0), np.arange(0, D, 2, dtype=np.float32) / np.float32(D))
    angle = (np.arange(H, dtype=np.float32)[:, None] * theta.astype(np.float32)[None, :]).astype(np.float32)
    tables = {n: np.ascontiguousarray(np.broadcast_to(np.tile(f(angle).astype(np.float32).reshape(1, -1), (1, 2)),
                                                      (P, C)))
              for n, f in (("rope_cos", np.cos), ("rope_sin", np.sin))}
    arrays = {
        "x": np.asarray(inputs["L0_attn_x"]),
        "w_attn": np.asarray(inputs["L0_attn_W_attn"]),
        "b_attn": np.asarray(inputs["L0_attn_b_attn"]).reshape(1, -1),
        "w_proj": np.asarray(inputs["L0_attn_W_proj"]),
        "b_proj": np.asarray(inputs["L0_attn_b_proj"]).reshape(1, -1),
        "w_gate_t": np.asarray(inputs["L0_ffn_w_gate"]).T,
        "w_up_t": np.asarray(inputs["L0_ffn_w_up"]).T,
        "w_down_t": np.asarray(inputs["L0_ffn_w_down"]).T,
        **tables,
    }
    nc = _bacc.Bacc("TRN2", target_bir_lowering=False, num_devices=1)
    maps, args = {}, []
    for name, a in arrays.items():
        a = np.ascontiguousarray(a)
        maps[f"in_{name}"] = a
        args.append(nc.dram_tensor(f"in_{name}", a.shape, _mybir.dt.from_np(a.dtype), kind="ExternalInput").ap())
    shape, dtype = _OUT
    out = nc.dram_tensor("out_0", shape, _mybir.dt.from_np(np.dtype(dtype)), kind="ExternalOutput").ap()
    build_program(nc, *args, out)
    r = _run(nc, [maps], core_ids=[0])
    return r.results[0]["out_0"]
```

```python
import numpy as np
import concourse.bass as bass
from concourse import mybir
from contextlib import ExitStack

B, T, C, H, D, HID = 8, 1024, 256, 16, 16, 768
P = 128
TT = T // P
GROUPS, GH = 4, 4
STEPS = 12
CH = 512
PARTS = 6
MROW = PARTS * D
LEAD = 16
NST, NMX, NP = 2, 3, 2 * GH
Q_PART = (0, 0, 1, 0, 1, 2)
K_PART = (0, 1, 0, 2, 1, 0)
XS = 2048.0
QSCALE = 1.0 / 127.0
EPS = 1e-5
NEG = -3.0e38

BLOCKS = [(0, k) for k in range(4)] + [(1, k) for k in range(8)]


def width(n):
    qc, kb = BLOCKS[n]
    return (qc + 1) * CH - max(qc * CH, kb * P)


def is_diag(n):
    qc, kb = BLOCKS[n]
    return kb >= 4 * qc


def pieces(s):
    if s < 4:
        return [(j, s, 0, P * (s + 1), True) for j in range(GH)]
    t, sub = 4 + (s - 4) // 2, (s - 4) % 2
    out = []
    for j in (2 * sub, 2 * sub + 1):
        out += [(j, t, 0, CH, False), (j, t, CH, P * (t - 3), True)]
    return out


TASKS = {
    (0, 0): [("XH", 0, 0)],
    (0, 1): [("QK", 1, 0, 0)],
    (0, 2): [("QK", 1, 0, 1)],
    (0, 4): [("QK", 1, 1, 0)],
    (0, 5): [("QK", 1, 1, 1)],
    (0, 7): [("XH", 1, 0)],
    (0, 10): [("YT", 3, 1)],
    (0, 12): [("FIN_T", 2)],
    (0, 14): [("FIN_T", 3)],
    (0, 16): [("YT", 0, 0), ("FIN_P", 2)],
    (0, 18): [("XH", 0, 1)],
    (0, 19): [("MT", 1)],
    (0, 20): [("V", 1, 0)],
    (0, 21): [("FIN_P", 3)],
    (0, 22): [("XH", 1, 1), ("UP", 0, 0), ("FIN_O", 2)],
    (0, 23): [("V", 1, 1)],
    (1, 1): [("LNS", 0), ("FIN_O", 3), ("UP", 0, 1)],
    (1, 3): [("YT", 0, 1), ("LNS", 1)],
    (1, 4): [("UP", 0, 2), ("LNS", 2)],
    (1, 5): [("UP", 0, 3)],
    (1, 8): [("LNS", 3)],
    (1, 9): [("LNR",), ("UP", 0, 4)],
    (1, 11): [("UP", 0, 5), ("LNA", 0)],
    (1, 12): [("LNA", 1)],
    (1, 13): [("LNA", 2), ("YT", 1, 0)],
    (1, 14): [("DN", 0, 0), ("LNA", 3)],
    (1, 18): [("TX", 0, 0), ("MT", 2)],
    (1, 19): [("TX", 1, 0)],
    (1, 22): [("TX", 0, 1)],
    (1, 23): [("TX", 1, 1)],
    (2, 0): [("QK", 0, 0, 0), ("QK", 0, 0, 1)],
    (2, 1): [("QK", 0, 1, 0), ("QK", 0, 1, 1)],
    (2, 2): [("DN", 0, 1)],
    (2, 4): [("V", 0, 0)],
    (2, 8): [("V", 0, 1)],
    (2, 9): [("YT", 1, 1)],
    (2, 10): [("UP", 1, 0)],
    (2, 12): [("YT", 2, 0)],
    (2, 17): [("MT", 3)],
    (2, 18): [("UP", 1, 1)],
    (3, 0): [("UP", 1, 2)],
    (3, 1): [("UP", 1, 3)],
    (3, 4): [("UP", 1, 4)],
    (3, 6): [("YT", 2, 1)],
    (3, 10): [("UP", 1, 5)],
    (3, 11): [("YT", 3, 0)],
    (3, 14): [("FIN_T", 0)],
    (3, 16): [("FIN_P", 0)],
    (3, 18): [("FIN_T", 1)],
    (3, 19): [("MT", 0)],
    (3, 20): [("FIN_O", 0), ("FIN_P", 1), ("FIN_O", 1)],
    (3, 21): [("DN", 1, 0)],
    (3, 22): [("DN", 1, 1)],
}
HALVES = 2 * STEPS
PRO = ([("LNS", p) for p in range(4)] + [("LNR",)] + [("LNA", p) for p in range(4)]
       + [("TX", 0, 0), ("TX", 1, 0), ("TX", 0, 1), ("TX", 1, 1)]
       + [("QK", 0, 0, 0), ("QK", 0, 0, 1), ("QK", 0, 1, 0), ("QK", 0, 1, 1), ("V", 0, 0), ("V", 0, 1)]
       + [("MT", 0)])
EPI = [("YT", 3, 1), ("FIN_T", 2), ("FIN_T", 3), ("FIN_P", 2), ("FIN_P", 3), ("FIN_O", 2), ("FIN_O", 3)]


def of_next(task):
    return task[0] in ("LNS", "LNR", "LNA", "TX") or task[:2] in (("QK", 0), ("V", 0)) or task == ("MT", 0)


def of_last(g, task):
    return task in (("FIN_T", 2), ("FIN_T", 3), ("FIN_P", 2), ("FIN_P", 3), ("FIN_O", 2), ("FIN_O", 3),
                    ("YT", 3, 1))


def tasks_at(kind, g, h):
    return [t for t in TASKS.get((g, h), [])
            if not (kind == "first" and of_last(g, t)) and not (kind == "last" and of_next(t))]


LAG = {
    "scalar": {"XH": 0, "TX": 0, "QK": 0, "UP": 0, "DN": 1, "FIN_T": 1, "MT": 0, "HI": 2},
    "vector": {"XH": 2, "QK": 1, "DN": 1, "FIN_O": 0, "LNS": 0, "LNR": 1, "V": 0, "UP": 0, "YT": 0, "FIN_P": 0},
    "gpsimd": {"LNA": 1, "QK": 2, "FIN_P": 1, "UP": 2},
    "sync": {"QK": 0, "MT": 0, "YT": 0, "FIN_O": 0},
}


def parts_at(engine, kind, g, h):
    lag = LAG[engine]
    found = []
    for late in range(max(lag.values()), -1, -1):
        at = HALVES * g + h - late
        if at >= 0:
            for t in tasks_at(kind, *divmod(at, HALVES)):
                if lag.get(t[0]) == late:
                    found.append(t)
                if t[0] == "UP" and lag.get("HI") == late:
                    found.append(("HI",) + t[1:])
    return found


def parts_of(engine, tasks):
    return [t for t in tasks if t[0] in LAG[engine]]


for _lags in LAG.values():
    for (_g, _h), _tasks in TASKS.items():
        for _t in _tasks:
            assert HALVES * _g + _h + max(_lags.get(_t[0], 0), _lags.get("HI", 0) * (_t[0] == "UP")) < HALVES * GROUPS

ORDER = {"pro": PRO, "epi": EPI}
for _kind in ("first", "mid", "last"):
    ORDER[_kind] = [t for g in range(GROUPS) for h in range(HALVES)
                    for t in tasks_at(_kind, g, h)]


class Tally:

    def __init__(self, events):
        self.seen = {k: [e for t in ORDER[k] for e in events(k, t)] for k in ORDER}
        n = {k: len(v) for k, v in self.seen.items()}
        self.base = {"pro": 0, "first": n["pro"], "mid": n["pro"] + n["first"]}
        self.each = n["mid"]
        self.base["last"] = self.base["mid"] + (B - 2) * self.each
        self.base["epi"] = self.base["last"] + n["last"]

    def at(self, kind, i, event):
        k = self.base[kind] + self.seen[kind].index(event) + 1
        return k + (i - 1) * self.each if kind == "mid" else k


def bank_uses():
    of = {}
    for kind in ("pro", "mid", "epi"):
        n = 0
        for t in ORDER[kind]:
            names = {"UP": ("gate", "up"), "LNS": (), "LNR": (), "LNA": (), "XH": (), "FIN_O": ()}.get(t[0], ("",))
            for name in names:
                of[kind, t, name] = n % 2
                n += 1
    for kind in ("first", "last"):
        of.update({(kind, t, name): b for (k, t, name), b in of.items() if k == "mid" and t in ORDER[kind]})
    return of


BANK = bank_uses()
HID_SCALE = 0.25 * QSCALE ** 2 / XS ** 2
FFN_SCALE = 2 * QSCALE
NEWTON = 3
LN_EACH = 2 * TT + 3 + 3 * NEWTON

USES = [Tally(lambda k, t, b=b: [(t, name) for name in ("", "gate", "up") if BANK.get((k, t, name)) == b])
        for b in range(2)]
BY = {name: Tally(lambda k, t, name=name: [t] if t[0] in name.split("+") else [])
      for name in ("TX", "XH", "QK", "UP+DN", "UP", "LNA", "YT", "FIN_P", "FIN_O", "MT")}


def tanh_before(kind, i, task):
    seen = BY["UP+DN"].seen[kind]
    k = seen.index(task) - 2
    if k >= 0:
        return kind, i, seen[k]
    return None if kind == "first" else ("mid", i - 1, seen[k])


def th_buffer(kind, task):
    return BY["UP+DN"].seen[kind].index(task) % 2


def tx_of(kind, i, task):
    tx = ("TX",) + task[1:]
    if kind == "first":
        return "pro", 0, tx
    if kind == "last":
        return "mid", B - 2, tx
    return "mid", i - 1, tx


def ln_number(kind, i):
    return 0 if kind == "pro" else i + 1


def diag_count(i, g, n):
    return 2 * GH * (GROUPS * i + g) + (n if n < 4 else n - 4) + 1


def wait(eng, sem, count):
    if isinstance(count, int) and count <= 0:
        return
    eng.wait_ge(sem, count)


def stand(eng, sem):
    eng.sem_inc(sem, 1)


def build_program(nc, x, w_attn, b_attn, w_proj, b_proj, w_gate_t, w_up_t, w_down_t, rope_cos, rope_sin, out):
    fp32, bf16, fp16, i32 = mybir.dt.float32, mybir.dt.bfloat16, mybir.dt.float16, mybir.dt.int32
    ALU, ACT, AX = mybir.AluOpType, mybir.ActivationFunctionType, mybir.AxisListType

    parts_dram = nc.dram_tensor("parts_scratch", (2, 2, 3, P, T), bf16).ap()
    mrow_dram = nc.dram_tensor("maxima_scratch", (GROUPS, 3 * GH, T), bf16).ap()
    bias_dram = nc.dram_tensor("bias_scratch", (1, 2 * C), fp32).ap()
    x_tiles = x.rearrange("b (t p) c -> b p t c", p=P)
    out_tiles = out.rearrange("b (t p) c -> b p t c", p=P)

    with ExitStack() as ctx:
        def sb(name, shape, dt):
            return ctx.enter_context(nc.sbuf_tensor(name, shape, dt))

        def sem(name):
            return ctx.enter_context(nc.semaphore(name))

        w_qkv = sb("w_qkv", [P, 2, 3 * C], fp32)
        w_pr = sb("w_pr", [P, 2, C], fp32)
        w_ga = sb("w_ga", [P, 2, HID], bf16)
        w_up = sb("w_up", [P, 2, HID], bf16)
        w_dn = sb("w_dn", [P, HID // P, C], bf16)
        b_row = sb("b_row", [1, 2 * C], fp32)
        b_qk = sb("b_qk", [P, 4], fp32)
        b_v = sb("b_v", [P, C], fp32)
        b_pr = sb("b_pr", [P, C], fp32)
        ident = sb("ident", [P, P], fp32)
        ident16 = sb("ident16", [P, P], bf16)
        tri = sb("tri", [P, CH], bf16)
        parts = sb("parts", [P, 2, 3, T], bf16)
        xn = parts[:, :, :, :].rearrange("p a b t -> p (a b t)")[:, 0:2 * TT * C].bitcast(fp32)\
            .rearrange("p (t c) -> p t c", c=C)
        xnT = sb("xnT", [P, 2, T], fp32)
        xh = sb("xh", [P, 2, T], fp16)
        xl = sb("xl", [P, 2, T], fp16)
        qkf = sb("qkf", [P, 2, CH], fp32)
        qkr = sb("qkr", [P, 2, CH], fp32)
        q_st = sb("q_st", [P, GROUPS, GH, T], bf16)
        k_st = sb("k_st", [P, GROUPS, GH, T], bf16)
        v_pad = sb("v_pad", [P, TT, H, D + 1], fp32)
        pexp = sb("pexp", [P, NP, CH], fp32)
        yT = sb("yT", [P, 2, CH], fp32)
        yn = sb("yn", [P, TT, C], fp32)
        ynT = sb("ynT", [P, 2, 2, 2 * P], fp32)
        yrec = sb("yrec", [P, 2, 4 * GH], fp32)
        mx_a = sb("mx_a", [P, 2, GH, TT], fp32)
        mx_b = sb("mx_b", [P, 2, GH, TT // 2], fp32)
        mx_r = sb("mx_r", [P, GH, TT], fp32)
        mx_p = sb("mx_p", [P, TT, 3, GH], bf16)
        mT = sb("mT", [3 * GH, T], bf16)
        junk = sb("junk", [P, GH, CH], bf16)
        hT = sb("hT", [P, 2, HID // P, CH], fp16)
        th = sb("th", [P, 2, CH], fp32)
        gu = sb("gu", [P, 2, CH], fp32)
        g2 = sb("g2", [P, TT, C], fp32)
        cosb = g2[:, 0, :].rearrange("p (a n) -> p a n", a=2)
        sinb = g2[:, 1, :].rearrange("p (a n) -> p a n", a=2)
        xo = sb("xo", [P, 2, 2, C], fp32)
        so = sb("so", [P, 2, 2 * C], fp32)
        ln6 = sb("ln6", [P, TT, 6], fp32)
        lnv = sb("lnv", [P, TT, 2], fp32)
        lne = sb("lne", [P, TT], fp32)
        lnt = sb("lnt", [P, TT], fp32)
        rstd = sb("rstd", [P, TT], fp32)
        st = ctx.enter_context(nc.psum_tensor("st", [P, NST, CH], fp32))
        mx = ctx.enter_context(nc.psum_tensor("mx", [P, NMX, CH], fp32))
        acc = ctx.enter_context(nc.psum_tensor("acc", [P, CH], fp32))
        tb = ctx.enter_context(nc.psum_tensor("tb", [P, 2, CH], fp32))

        x_in = sem("x_in")
        w_in = {n: sem("w_in_" + n) for n in ("attn", "rope", "bias", "proj", "gate", "up", "down", "bias_v", "rest")}
        w_ready = sem("w_ready")
        w_chain = sem("w_chain")
        b_chain = sem("b_chain")
        b_turned = sem("b_turned")
        b_back = sem("b_back")
        const_ready = sem("const_ready")
        ones_ready = sem("ones_ready")
        ln_chain = sem("ln_chain")
        xn_ready = sem("xn_ready")
        xh_ready = sem("xh_ready")
        xl_ready = sem("xl_ready")
        task_ready = [sem(f"task_ready{b}") for b in range(2)]
        task_free = [sem(f"task_free{b}") for b in range(2)]
        qk_first = sem("qk_first")
        qk_rest = sem("qk_rest")
        qk_second = sem("qk_second")
        qk_third = sem("qk_third")
        parts_out = [sem("q_parts_out"), sem("k_parts_out")]
        stack_in = [sem(f"stack_in{g}") for g in range(GROUPS)]
        mx_ready = sem("mx_ready")
        mx_done = sem("mx_done")
        mp_chain = sem("mp_chain")
        mrow_out = sem("mrow_out")
        mrow_in = [sem(f"mrow_in{g}") for g in range(GROUPS)]
        st_ready = sem("st_ready")
        exp_done = sem("exp_done")
        tri_done = sem("tri_done")
        pv_done = sem("pv_done")
        acc_out = sem("acc_out")
        yrec_ready = sem("yrec_ready")
        const0 = sem("const0")
        h_high = sem("h_high")
        h_low = sem("h_low")
        th_ready = sem("th_ready")
        so_scaled = sem("so_scaled")
        xo_in = [sem(f"xo_in{b}") for b in range(2)]
        o_ready = sem("o_ready")
        o_out = [sem(f"o_out{b}") for b in range(2)]

        dve_stand, pool_stand, sp_stand = sem("dve_stand"), sem("pool_stand"), sem("sp_stand")

        block = ctx.enter_context(nc.Block())

        def turn(eng, we, wo, cos, sin, tmp, chain):
            for dst, a, b in ((tmp[0], we, cos), (tmp[1], wo, sin), (tmp[2], wo, cos), (tmp[3], we, sin)):
                last = eng.tensor_tensor(dst, a, b, ALU.mult)
            last.then_inc(chain, 1)
            eng.wait_ge(chain, 1)
            eng.tensor_tensor(we, tmp[0], tmp[1], ALU.subtract)
            return eng.tensor_tensor(wo, tmp[2], tmp[3], ALU.add)

        def normalise(eng, p):
            for tt in (2 * p, 2 * p + 1):
                ins = eng.tensor_scalar(xn[:, tt, :], xn[:, tt, :], lnv[:, tt, 0:1], rstd[:, tt:tt + 1],
                                        ALU.subtract, ALU.mult)
            ins.then_inc(xn_ready, 1)

        def bank(kind, task, name=""):
            return BANK[kind, task, name]

        def use(kind, i, task, name=""):
            return USES[bank(kind, task, name)].at(kind, i, (task, name))

        def wait_ready(eng, kind, i, task, name=""):
            eng.wait_ge(task_ready[bank(kind, task, name)], use(kind, i, task, name))

        def wait_done(eng, kind, i, task, name=""):
            eng.wait_ge(task_free[bank(kind, task, name)], use(kind, i, task, name))

        def run(engine, body, prologue, epilogue):
            prologue()
            body("first", 0)
            with engine.Fori(1, B - 1) as i:
                body("mid", i)
            body("last", B - 1)
            epilogue()

        def max_steps(kind, i, g, n):
            ahead = STEPS * g + n + LEAD
            du, s = divmod(ahead, STEPS)
            if kind == "last" and du >= GROUPS:
                return None
            return 4 * i + du, du % GROUPS, s

        w_raw = {
            "gate": hT[:, 0, :, :].rearrange("p m n -> p (m n)").bitcast(i32).rearrange("p (k n) -> p k n", k=2),
            "up": hT[:, 1, :, :].rearrange("p m n -> p (m n)").bitcast(i32).rearrange("p (k n) -> p k n", k=2),
            "down": yn[:, :, :].rearrange("p t c -> p (t c)")[:, 0:6 * C].bitcast(i32)
                .rearrange("p (k n) -> p k n", k=6),
        }

        @block.sync
        def _(sp):
            def store_parts(kind, i, hf, which):
                sp.wait_ge(qk_third, BY["QK"].at(kind, i, ("QK", hf, which, 1)))
                sp.dma_start(parts_dram[hf, which].rearrange("a p n -> p a n"),
                             parts[:, which, :, :]).then_inc(parts_out[which], 16)

            def load_stacks(i, hf):
                for g in (2 * hf, 2 * hf + 1):
                    for which, stack, part_of in ((0, q_st, Q_PART), (1, k_st, K_PART)):
                        sp.wait_ge(parts_out[which], 16 * (2 * i + hf + 1))
                        stand(sp, sp_stand)
                        wait(sp, st_ready, STEPS * GH * (4 * i + g - GROUPS + 1))
                        for s in range(PARTS):
                            src = parts_dram[hf, which, part_of[s], 64 * (g % 2):64 * (g % 2) + 64, :]
                            sp.dma_start(stack[D * s:D * s + D, g, :, :],
                                         src.rearrange("(j d) n -> d j n", d=D)).then_inc(stack_in[g], 16)

            def load_x(i):
                stand(sp, sp_stand)
                sp.dma_start(xn, batch(x_tiles, i)).then_inc(x_in, 16)

            def batch(tiles, i):
                if isinstance(i, int):
                    return tiles[i]
                return tiles[bass.ds(i, 1)].rearrange("b p t c -> p (b t) c")

            def store_maxima(kind, i, g):
                wait_done(sp, kind, i, ("MT", g))
                sp.dma_start(mrow_dram[g], mT[:, :]).then_inc(mrow_out, 16)
                sp.wait_ge(mrow_out, 16 * BY["MT"].at(kind, i, ("MT", g)))
                sp.dma_start(q_st[MROW:MROW + 3, g, :, :],
                             mrow_dram[g].rearrange("(a j) n -> a j n", a=3)).then_inc(mrow_in[g], 16)

            def load_xo(kind, i, tp):
                buf = tp % 2
                wait(sp, o_out[buf], 16 * (2 * i + tp // 2))
                stand(sp, sp_stand)
                sp.dma_start(xo[:, buf, :, :], batch(x_tiles, i)[:, 2 * tp:2 * tp + 2, :]).then_inc(xo_in[buf], 16)

            def store_out(kind, i, tp, done_of):
                buf = tp % 2
                sp.wait_ge(o_ready, BY["FIN_O"].at(kind, i, ("FIN_O", tp)))
                stand(sp, sp_stand)
                sp.dma_start(batch(out_tiles, done_of)[:, 2 * tp:2 * tp + 2, :], xo[:, buf, :, :])\
                    .then_inc(o_out[buf], 16)

            def task(kind, i, g, t):
                if t[0] == "QK" and t[3] == 1:
                    store_parts(kind, i, t[1], t[2])
                    if t[2] == 1:
                        load_stacks(i if t[1] else i + 1, t[1])
                    if t == ("QK", 1, 1, 1) and kind != "last":
                        load_x(i + 1)
                if t[0] == "MT":
                    store_maxima(kind, i, t[1])
                if t == ("YT", 2, 1):
                    load_xo(kind, i, 0)
                    load_xo(kind, i, 1)
                if t[0] == "FIN_O":
                    store_out(kind, i, t[1], i if t[1] < 2 else i - 1)
                    if t[1] < 2:
                        load_xo(kind, i, t[1] + 2)

            def prologue():
                load_x(0)
                sp.dma_start(b_row[:, :], b_attn[:, 0:2 * C]).then_inc(w_in["bias"], 16)
                sp.dma_start(cosb, rope_cos.rearrange("p (a n) -> p a n", a=2)).then_inc(w_in["rope"], 16)
                sp.dma_start(sinb, rope_sin.rearrange("p (a n) -> p a n", a=2)).then_inc(w_in["rope"], 16)
                sp.dma_start(w_qkv[:, :, :], w_attn.rearrange("(k p) n -> p k n", p=P)).then_inc(w_in["attn"], 16)
                sp.wait_ge(b_turned, 1)
                sp.dma_start(bias_dram, b_row[:, :]).then_inc(b_back, 16)
                sp.wait_ge(b_back, 16)
                sp.dma_start(b_qk[:, :], bias_dram.rearrange("o (t p) -> p (o t)", p=P),
                             allow_slow_non_contiguous=True).then_inc(b_back, 16)
                sp.dma_start(b_v[:, :], b_attn[:, 2 * C:3 * C].broadcast_to([P, C])).then_inc(w_in["bias_v"], 16)
                store_parts("pro", 0, 0, 0)
                store_parts("pro", 0, 0, 1)
                load_stacks(0, 0)
                sp.dma_start(b_pr[:, :], b_proj.broadcast_to([P, C])).then_inc(w_in["rest"], 16)
                sp.dma_start(w_pr[:, :, :], w_proj.rearrange("(k p) n -> p k n", p=P)).then_inc(w_in["proj"], 16)
                sp.dma_start(w_raw["gate"], w_gate_t.rearrange("(k p) n -> p k n", p=P)).then_inc(w_in["gate"], 16)
                sp.dma_start(w_raw["up"], w_up_t.rearrange("(k p) n -> p k n", p=P)).then_inc(w_in["up"], 16)
                sp.dma_start(w_raw["down"], w_down_t.rearrange("(k p) n -> p k n", p=P)).then_inc(w_in["down"], 16)
                store_maxima("pro", 0, 0)

            def body(kind, i):
                for g in range(GROUPS):
                    for h in range(HALVES):
                        for t in parts_at("sync", kind, g, h):
                            task(kind, i, g, t)

            def epilogue():
                for t in parts_of("sync", EPI):
                    task("epi", B, 0, t)
                for buf in range(2):
                    sp.wait_ge(o_out[buf], 16 * 2 * B)

            run(sp, body, prologue, epilogue)

        @block.tensor
        def _(pe):
            def take(kind, i, task, name=""):
                b = bank(kind, task, name)
                wait(pe, task_free[b], use(kind, i, task, name) - 1)
                return tb[:, b, :], task_ready[b]

            def scores(i, g, n, j):
                qc, kb = BLOCKS[n]
                w = width(n)
                index = STEPS * GH * (4 * i + g) + GH * n + j
                wait(pe, exp_done, index - NST + 1)
                if n == 0 and j == 0:
                    pe.wait_ge(mrow_in[g], 16 * (i + 1))
                q0 = (qc + 1) * CH - w
                nc.tensor.matmul(st[:, (GH * n + j) % NST, 0:w], k_st[0:MROW + 3, g, j, kb * P:(kb + 1) * P],
                                 q_st[0:MROW + 3, g, j, q0:q0 + w], start=True, stop=True).then_inc(st_ready, 1)

            def max_piece(unit, g, s, c, i_next):
                j, t, k0, w, _ = pieces(s)[c]
                if s == 0 and c == 0:
                    pe.wait_ge(stack_in[g], 16 * 2 * PARTS * (i_next + 1))
                index = (STEPS * unit + s) * GH + c
                wait(pe, mx_done, index - NMX + 1)
                nc.tensor.matmul(mx[:, (GH * s + c) % NMX, 0:w], q_st[0:MROW, g, j, t * P:(t + 1) * P],
                                 k_st[0:MROW, g, j, k0:k0 + w], start=True, stop=True).then_inc(mx_ready, 1)

            def values(i, g, n, pair):
                qc, kb = BLOCKS[n]
                w = width(n)
                if pair == 0:
                    if is_diag(n):
                        pe.wait_ge(tri_done, diag_count(i, g, n))
                    else:
                        pe.wait_ge(exp_done, GH * (STEPS * (4 * i + g) + n + 1))
                    if kb == 0:
                        wait(pe, acc_out, 2 * (4 * i + g) + qc)
                for j in (2 * pair, 2 * pair + 1):
                    mm = nc.tensor.matmul(acc[32 * j:32 * j + D + 1, CH - w:CH], v_pad[:, kb, GH * g + j, :],
                                          pexp[:, GH * (n % 2) + j, 0:w],
                                          start=kb == 0, stop=kb == 4 * qc + 3)
                mm.then_inc(pv_done, 1)

            def task(kind, i, g, t):
                if t[0] == "TX":
                    _, kt, c = t
                    pe.wait_ge(xn_ready, BY["LNA"].at(kind, i, ("LNA", 2 * c + 1)))
                    dst, ready = take(kind, i, t)
                    for tt in range(4):
                        mm = nc.tensor.transpose(dst[:, tt * P:(tt + 1) * P],
                                                 xn[:, 4 * c + tt, kt * P:(kt + 1) * P], ident[:, :])
                    mm.then_inc(ready, 1)
                if t[0] == "QK":
                    _, hf, which, c = t
                    if hf == 0 and which == 0:
                        for kt in range(2):
                            wait_done(pe, kind, i, ("TX", kt, c))
                    dst, ready = take(kind, i, t)
                    col = which * C + hf * P
                    for kt in range(2):
                        mm = nc.tensor.matmul(dst, w_qkv[:, kt, col:col + P], xnT[:, kt, c * CH:(c + 1) * CH],
                                              start=kt == 0, stop=kt == 1)
                    mm.then_inc(ready, 1)
                if t[0] == "V":
                    _, hf, tq = t
                    dst, ready = take(kind, i, t)
                    for tt in range(4):
                        for kt in range(2):
                            mm = nc.tensor.matmul(dst[:, tt * P:(tt + 1) * P],
                                                  xnT[:, kt, (4 * tq + tt) * P:(4 * tq + tt + 1) * P],
                                                  w_qkv[:, kt, 2 * C + hf * P:2 * C + hf * P + P],
                                                  start=kt == 0, stop=kt == 1)
                    mm.then_inc(ready, 1)
                if t[0] == "UP":
                    _, c, m = t
                    if m == 0:
                        pe.wait_ge(xl_ready, BY["XH"].at(kind, i, ("XH", 1, c)))
                    for name, w in (("gate", w_ga), ("up", w_up)):
                        dst, ready = take(kind, i, t, name)
                        for kt in range(2):
                            for xpart in (xh, xl):
                                mm = nc.tensor.matmul(dst, w[:, kt, m * P:(m + 1) * P],
                                                      xpart[:, kt, c * CH:(c + 1) * CH],
                                                      start=kt == 0 and xpart is xh, stop=kt == 1 and xpart is xl)
                        mm.then_inc(ready, 1)
                if t[0] == "DN":
                    _, c, tp = t
                    if tp == 0:
                        pe.wait_ge(h_low, BY["UP"].at(kind, i, ("UP", c, HID // P - 1)))
                    dst, ready = take(kind, i, t)
                    for t2 in range(2):
                        for m in range(HID // P):
                            for low in range(2):
                                mm = nc.tensor.matmul(dst[:, t2 * C:(t2 + 1) * C],
                                                      hT[:, low, m, (2 * tp + t2) * P:(2 * tp + t2 + 1) * P],
                                                      w_dn[:, m, :], start=m == 0 and not low,
                                                      stop=m == HID // P - 1 and low == 1)
                    mm.then_inc(ready, 1)
                if t[0] == "YT":
                    _, yg, qc = t
                    unit_i = i - 1 if (yg, qc) == (3, 1) else i
                    pe.wait_ge(acc_out, 2 * (4 * unit_i + yg) + qc + 1)
                    dst, ready = take(kind, i, t)
                    for tt in range(4):
                        mm = nc.tensor.transpose(dst[:, tt * P:(tt + 1) * P], yT[:, qc, tt * P:(tt + 1) * P],
                                                 ident[:, :])
                    mm.then_inc(ready, 1)
                if t[0] == "FIN_T":
                    _, tp = t
                    if tp in (0, 2):
                        wait_done(pe, kind, i, ("YT", 3, tp // 2))
                    dst, ready = take(kind, i, t)
                    for kt in range(2):
                        for t2 in range(2):
                            mm = nc.tensor.transpose(dst[:, kt * 2 * P + t2 * P:kt * 2 * P + (t2 + 1) * P],
                                                     yn[:, 2 * tp + t2, kt * P:(kt + 1) * P], ident[:, :])
                    mm.then_inc(ready, 1)
                if t[0] == "FIN_P":
                    _, tp = t
                    wait_done(pe, kind, i, ("FIN_T", tp))
                    dst, ready = take(kind, i, t)
                    for t2 in range(2):
                        for kt in range(2):
                            mm = nc.tensor.matmul(dst[:, t2 * C:(t2 + 1) * C],
                                                  ynT[:, tp % 2, kt, t2 * P:(t2 + 1) * P], w_pr[:, kt, :],
                                                  start=kt == 0, stop=kt == 1)
                    mm.then_inc(ready, 1)
                if t[0] == "MT":
                    pe.wait_ge(mp_chain, 5 * BY["MT"].at(kind, i, t))
                    dst, ready = take(kind, i, t)
                    for tt in range(TT):
                        mm = nc.tensor.transpose(dst[0:3 * GH, :].bitcast(bf16)[:, tt * P:(tt + 1) * P],
                                                 mx_p[:, tt, :, :].rearrange("p a j -> p (a j)"), ident16[:, :])
                    mm.then_inc(ready, 1)

            def prologue():
                pe.wait_ge(const_ready, 2)
                for t in PRO[:-1]:
                    if t == ("QK", 0, 0, 0):
                        pe.wait_ge(w_ready, 1)
                    task("pro", 0, 0, t)
                for ahead in range(LEAD):
                    unit, s = divmod(ahead, STEPS)
                    for c in range(GH):
                        max_piece(unit, unit, s, c, 0)
                    if ahead == STEPS:
                        task("pro", 0, 0, ("MT", 0))
                pe.wait_ge(w_ready, 4)
                pe.wait_ge(const_ready, 5)
                pe.wait_ge(w_in["proj"], 16)
                for tq in range(2):
                    wait_done(pe, "pro", 0, ("V", 0, tq))

            def body(kind, i):
                for g in range(GROUPS):
                    for n in range(STEPS):
                        ahead = max_steps(kind, i, g, n)
                        i_next = i + (STEPS * g + n + LEAD) // (STEPS * GROUPS)
                        if ahead:
                            unit, mg, s = ahead
                        for half in range(2):
                            scores(i, g, n, 2 * half)
                            if ahead:
                                max_piece(unit, mg, s, 2 * half, i_next)
                            scores(i, g, n, 2 * half + 1)
                            back = STEPS * g + n - 2 + half
                            if back >= 0:
                                values(i, *divmod(back, STEPS), 1 - half)
                            elif kind != "first":
                                values(i - 1, *divmod(back + STEPS * GROUPS, STEPS), 1 - half)
                            if ahead:
                                max_piece(unit, mg, s, 2 * half + 1, i_next)
                            for t in tasks_at(kind, g, 2 * n + half):
                                task(kind, i, g, t)

            def epilogue():
                values(B - 1, GROUPS - 1, STEPS - 2, 1)
                values(B - 1, GROUPS - 1, STEPS - 1, 0)
                values(B - 1, GROUPS - 1, STEPS - 1, 1)
                for t in EPI:
                    task("epi", B, 0, t)

            run(pe, body, prologue, epilogue)

        @block.scalar
        def _(act):
            def exps(i, g, n, heads):
                w = width(n)
                for j in heads:
                    index = STEPS * GH * (4 * i + g) + GH * n + j
                    if j % 2 == 0:
                        before = 2 * (STEPS * (4 * i + g) + n - 2) + j // 2 + 1
                        if n >= 2 or g > 0 or not isinstance(i, int) or i > 0:
                            act.wait_ge(pv_done, before)
                    act.wait_ge(st_ready, index + 1)
                    nc.scalar.activation(pexp[:, GH * (n % 2) + j, 0:w], st[:, (GH * n + j) % NST, 0:w], ACT.Exp,
                                         scale=1.0 / np.sqrt(D)).then_inc(exp_done, 1)

            def copy_acc(i, g, qc):
                act.wait_ge(pv_done, 2 * (STEPS * (4 * i + g) + (4 if qc == 0 else STEPS)))
                nc.scalar.activation(yT[:, qc, :], acc[:, :], ACT.Copy).then_inc(acc_out, 1)

            def task(kind, i, g, t):
                if t[0] == "TX":
                    _, kt, c = t
                    wait_ready(act, kind, i, t)
                    nc.scalar.activation(xnT[:, kt, c * CH:(c + 1) * CH], tb[:, bank(kind, t), :], ACT.Copy)\
                        .then_inc(task_free[bank(kind, t)], 1)
                if t[0] == "XH":
                    _, kt, c = t
                    cols = slice(c * CH, (c + 1) * CH)
                    wait_done(act, *tx_of(kind, i, t))
                    nc.scalar.activation(xh[:, kt, cols], xnT[:, kt, cols], ACT.Copy, scale=XS).then_inc(xh_ready, 1)
                if t[0] == "QK":
                    _, hf, which, c = t
                    k = BY["QK"].at(kind, i, t)
                    src = tb[:, bank(kind, t), :]
                    bias = b_qk[:, 2 * which + hf:2 * which + hf + 1]
                    wait_ready(act, kind, i, t)
                    wait(act, qk_rest, k - 2)
                    nc.scalar.activation(qkf[:, c, :], src, ACT.Identity, bias=bias)
                    if kind != "pro":
                        act.wait_ge(parts_out[which], 16 * (2 * i + 2 - hf))
                    nc.scalar.activation(parts[:, which, 0, c * CH:(c + 1) * CH], src, ACT.Identity, bias=bias)\
                        .then_inc(task_free[bank(kind, t)], 1)
                if t[0] == "UP":
                    _, c, m = t
                    wait_ready(act, kind, i, t, "gate")
                    wait_th(kind, i, t)
                    nc.scalar.activation(th[:, th_buffer(kind, t), :], tb[:, bank(kind, t, "gate"), :],
                                         ACT.Tanh, scale=0.5 * QSCALE / XS).then_inc(th_ready, 1)
                if t[0] == "HI":
                    _, c, m = t
                    wait_done(act, kind, i, ("UP", c, m), "up")
                    nc.scalar.activation(hT[:, 0, m, :], gu[:, m % 2, :], ACT.Copy).then_inc(h_high, 1)
                if t[0] == "DN":
                    wait_ready(act, kind, i, t)
                    wait_th(kind, i, t)
                    nc.scalar.activation(th[:, th_buffer(kind, t), :], tb[:, bank(kind, t), :],
                                         ACT.Tanh, scale=0.5 * FFN_SCALE).then_inc(th_ready, 1)
                if t[0] == "FIN_T":
                    _, tp = t
                    wait_ready(act, kind, i, t)
                    b = bank(kind, t)
                    nc.scalar.activation(ynT[:, tp % 2, :, :], tb[:, b, :].rearrange("p (k n) -> p k n", k=2),
                                         ACT.Copy).then_inc(task_free[b], 1)
                if t[0] == "MT":
                    k = BY["MT"].at(kind, i, t)
                    b = bank(kind, t)
                    wait_ready(act, kind, i, t)
                    wait(act, mrow_out, 16 * (k - 1))
                    nc.scalar.activation(mT[:, :], tb[0:3 * GH, b, :].bitcast(bf16), ACT.Copy)\
                        .then_inc(task_free[b], 1)

            def wait_th(kind, i, t):
                before = tanh_before(kind, i, t)
                if before:
                    wait_done(act, *before, "gate" if before[2][0] == "UP" else "")

            def prologue():
                for t in parts_of("scalar", PRO):
                    if t == ("QK", 0, 0, 0):
                        act.wait_ge(b_back, 32)
                    task("pro", 0, 0, t)

            def body(kind, i):
                for g in range(GROUPS):
                    for n in range(STEPS):
                        for half in range(2):
                            exps(i, g, n, (2 * half, 2 * half + 1))
                            if half == 0 and n == 1 and (g > 0 or kind != "first"):
                                copy_acc(i if g else i - 1, (g - 1) % GROUPS, 1)
                            if half == 0 and n == 5:
                                copy_acc(i, g, 0)
                            for t in parts_at("scalar", kind, g, 2 * n + half):
                                task(kind, i, g, t)

            def epilogue():
                copy_acc(B - 1, GROUPS - 1, 1)
                for t in parts_of("scalar", EPI):
                    task("epi", B, 0, t)

            run(act, body, prologue, epilogue)

        @block.vector
        def _(dve):
            def max_take(unit, g, s, which=range(GH)):
                par = g % 2
                for c in which:
                    j, t, k0, w, diag = pieces(s)[c]
                    index = (STEPS * unit + s) * GH + c
                    dve.wait_ge(mx_ready, index + 1)
                    dst = mx_b[:, par, j, t - 4:t - 3] if k0 else mx_a[:, par, j, t:t + 1]
                    src = mx[:, (GH * s + c) % NMX, 0:w]
                    if diag:
                        stand(dve, dve_stand)
                        nc.vector.tensor_tensor_reduce(out=junk[:, c, 0:w], in0=src, in1=tri[:, CH - w:CH],
                                                       scale=1.0, scalar=NEG, op0=ALU.add, op1=ALU.max,
                                                       accum_out=dst).then_inc(mx_done, 1)
                    else:
                        nc.vector.reduce_max(dst, src, AX.X).then_inc(mx_done, 1)

            def mp_step(ins, count):
                ins.then_inc(mp_chain, 1)
                dve.wait_ge(mp_chain, count)

            def split_maxima(kind, i, t, unit):
                par = t[1] % 2
                base = 5 * (BY["MT"].at(kind, i, t) - 1)
                m = mx_a[:, par, :, :]
                m_t = mx_a[:, par, :, :].rearrange("p j t -> p t j")
                r_t = mx_r[:, :, :].rearrange("p j t -> p t j")
                dve.wait_ge(mx_done, STEPS * GH * (unit + 1))
                mp_step(nc.vector.tensor_tensor(m[:, :, 4:8], m[:, :, 4:8], mx_b[:, par, :, :], ALU.max), base + 1)
                wait(dve, mrow_out, 16 * (BY["MT"].at(kind, i, t) - 1))
                mp_step(nc.vector.tensor_scalar(mx_p[:, :, 0, :], m_t, -1.0, None, ALU.mult), base + 2)
                mp_step(nc.vector.scalar_tensor_tensor(out=r_t, in0=m_t, scalar=-1.0, in1=mx_p[:, :, 0, :],
                                                       op0=ALU.mult, op1=ALU.subtract), base + 3)
                mp_step(nc.vector.tensor_copy(mx_p[:, :, 1, :], r_t), base + 4)
                nc.vector.tensor_tensor(mx_p[:, :, 2, :], r_t, mx_p[:, :, 1, :], ALU.subtract).then_inc(mp_chain, 1)

            def ln_step(ins, kind, i, k):
                ins.then_inc(ln_chain, 1)
                dve.wait_ge(ln_chain, LN_EACH * ln_number(kind, i) + k)

            def task(kind, i, g, t):
                if t[0] == "LNS":
                    _, p = t
                    if p == 0:
                        dve.wait_ge(x_in, 16 * (ln_number(kind, i) + 1))
                    for tt in (2 * p, 2 * p + 1):
                        nc.vector.bn_stats(ln6[:, tt, :], xn[:, tt, :]).then_inc(ln_chain, 1)
                    dve.wait_ge(ln_chain, LN_EACH * ln_number(kind, i) + 4 * p + 2)
                    stand(dve, dve_stand)
                    for tt in (2 * p, 2 * p + 1):
                        nc.vector.bn_aggr(lnv[:, tt, :], ln6[:, tt, :]).then_inc(ln_chain, 1)
                if t[0] == "LNR":
                    k = 2 * TT
                    dve.wait_ge(ln_chain, LN_EACH * ln_number(kind, i) + k)
                    ln_step(nc.vector.tensor_scalar(lne[:, :], lnv[:, :, 1], EPS, None, ALU.add), kind, i, k + 1)
                    ln_step(nc.vector.tensor_scalar(rstd[:, :].bitcast(i32), lne[:, :].bitcast(i32), 1, None,
                                                    ALU.arith_shift_right), kind, i, k + 2)
                    ln_step(nc.vector.tensor_scalar(rstd[:, :].bitcast(i32), rstd[:, :].bitcast(i32), -1.0,
                                                    float(0x5F3759DF), ALU.mult, ALU.add), kind, i, k + 3)
                    for it in range(NEWTON):
                        k = 2 * TT + 3 + 3 * it
                        ln_step(nc.vector.tensor_tensor(lnt[:, :], rstd[:, :], rstd[:, :], ALU.mult), kind, i, k + 1)
                        ln_step(nc.vector.scalar_tensor_tensor(out=lnt[:, :], in0=lnt[:, :], scalar=-0.5,
                                                               in1=lne[:, :], op0=ALU.mult, op1=ALU.mult),
                                kind, i, k + 2)
                        ln_step(nc.vector.scalar_tensor_tensor(out=rstd[:, :], in0=lnt[:, :], scalar=1.5,
                                                               in1=rstd[:, :], op0=ALU.add, op1=ALU.mult),
                                kind, i, k + 3)
                if t[0] == "LNA":
                    normalise(nc.vector, t[1])
                if t[0] == "XH":
                    _, kt, c = t
                    cols = slice(c * CH, (c + 1) * CH)
                    dve.wait_ge(xh_ready, BY["XH"].at(kind, i, t))
                    nc.vector.scalar_tensor_tensor(out=xl[:, kt, cols], in0=xnT[:, kt, cols], scalar=XS,
                                                   in1=xh[:, kt, cols], op0=ALU.mult,
                                                   op1=ALU.subtract).then_inc(xl_ready, 1)
                if t[0] == "QK":
                    _, hf, which, c = t
                    k = BY["QK"].at(kind, i, t)
                    wait_done(dve, kind, i, t)
                    wait(dve, qk_third, k - 2)
                    part = parts[:, which, :, c * CH:(c + 1) * CH]
                    nc.vector.tensor_tensor(qkr[:, c, :], qkf[:, c, :], part[:, 0, :], ALU.subtract)\
                        .then_inc(qk_rest, 1)
                    dve.wait_ge(qk_rest, k)
                    nc.vector.tensor_copy(part[:, 1, :], qkr[:, c, :]).then_inc(qk_second, 1)
                if t[0] == "V":
                    _, hf, tq = t
                    b = bank(kind, t)
                    wait_ready(dve, kind, i, t)
                    nc.vector.tensor_tensor(
                        v_pad[:, 4 * tq:4 * tq + 4, 8 * hf:8 * hf + 8, 0:D],
                        tb[:, b, :].rearrange("p (t h d) -> p t h d", t=4, d=D),
                        b_v[:, hf * P:(hf + 1) * P].rearrange("p (o h d) -> p o h d", o=1, d=D)
                        .broadcast_to([P, 4, 8, D]), ALU.add).then_inc(task_free[b], 1)
                if t[0] == "UP":
                    _, c, m = t
                    k = BY["UP+DN"].at(kind, i, t)
                    ba, bb = bank(kind, t, "gate"), bank(kind, t, "up")
                    dve.wait_ge(th_ready, k)
                    wait(dve, h_low, BY["UP"].at(kind, i, t) - 2)
                    h = gu[:, m % 2, :]
                    nc.vector.scalar_tensor_tensor(out=h, in0=th[:, th_buffer(kind, t), :], scalar=1.0,
                                                   in1=tb[:, ba, :], op0=ALU.add, op1=ALU.mult)\
                        .then_inc(task_free[ba], 1)
                    wait_done(dve, kind, i, t, "gate")
                    wait_ready(dve, kind, i, t, "up")
                    nc.vector.scalar_tensor_tensor(out=h, in0=h, scalar=HID_SCALE, in1=tb[:, bb, :],
                                                   op0=ALU.mult, op1=ALU.mult).then_inc(task_free[bb], 1)
                if t[0] == "DN":
                    _, c, tp = t
                    b = bank(kind, t)
                    k = BY["UP+DN"].at(kind, i, t)
                    dve.wait_ge(th_ready, k)
                    if kind != "first" and (c, tp) == (1, 0):
                        dve.wait_ge(so_scaled, BY["FIN_P"].at(kind, i, ("FIN_P", 3)))
                    nc.vector.scalar_tensor_tensor(
                        out=g2[:, 4 * c + 2 * tp:4 * c + 2 * tp + 2, :].rearrange("p t c -> p (t c)"),
                        in0=th[:, th_buffer(kind, t), :], scalar=1.0, in1=tb[:, b, :],
                        op0=ALU.add, op1=ALU.mult).then_inc(task_free[b], 1)
                if t[0] == "YT":
                    _, yg, qc = t
                    b = bank(kind, t)
                    k = BY["YT"].at(kind, i, t)
                    wait_ready(dve, kind, i, t)
                    y4 = tb[:, b, :].rearrange("p (t j r) -> p t j r", t=4, r=32)
                    nc.vector.reciprocal(yrec[:, qc, :].rearrange("p (t j o) -> p t j o", t=4, o=1),
                                         y4[:, :, :, D:D + 1]).then_inc(yrec_ready, 1)
                    dve.wait_ge(yrec_ready, k)
                    nc.vector.tensor_tensor(
                        yn[:, 4 * qc:4 * qc + 4, yg * 64:yg * 64 + 64].rearrange("p t (j d) -> p t j d", d=D),
                        y4[:, :, :, 0:D],
                        yrec[:, qc, :].rearrange("p (t j o) -> p t j o", t=4, o=1).broadcast_to([P, 4, GH, D]),
                        ALU.mult).then_inc(task_free[b], 1)
                if t[0] == "FIN_P":
                    _, tp = t
                    b = bank(kind, t)
                    k = BY["FIN_P"].at(kind, i, t)
                    wait_ready(dve, kind, i, t)
                    wait(dve, o_ready, k - 2)
                    nc.vector.tensor_tensor(so[:, tp % 2, :].rearrange("p (t c) -> p t c", t=2),
                                            tb[:, b, :].rearrange("p (t c) -> p t c", t=2),
                                            b_pr[:, :].rearrange("p (o c) -> p o c", o=1).broadcast_to([P, 2, C]),
                                            ALU.add).then_inc(task_free[b], 1)
                if t[0] == "FIN_O":
                    _, tp = t
                    k = BY["FIN_O"].at(kind, i, t)
                    dve.wait_ge(so_scaled, k)
                    dve.wait_ge(xo_in[tp % 2], 16 * (2 * (i if tp < 2 else i - 1) + tp // 2 + 1))
                    o = xo[:, tp % 2, :, :].rearrange("p t c -> p (t c)")
                    nc.vector.scalar_tensor_tensor(out=o, in0=so[:, tp % 2, :], scalar=0.5 * FFN_SCALE, in1=o,
                                                   op0=ALU.mult, op1=ALU.add).then_inc(o_ready, 1)

            def prologue():
                nc.vector.memset(acc[:, :], 0.0)
                for t in PRO[:9]:
                    task("pro", 0, 0, t)
                for t in PRO[9:-1]:
                    if t[0] == "V" and t[2] == 0:
                        dve.wait_ge(w_in["bias_v"], 16)
                        dve.wait_ge(ones_ready, 2)
                    task("pro", 0, 0, t)
                dve.wait_ge(const_ready, 4)
                for ahead in range(LEAD):
                    unit, s = divmod(ahead, STEPS)
                    if ahead == STEPS:
                        split_maxima("pro", 0, ("MT", 0), 0)
                    max_take(unit, unit, s)
                dve.wait_ge(w_in["rest"], 16)
                dve.wait_ge(w_ready, 4)

            def body(kind, i):
                for g in range(GROUPS):
                    for n in range(STEPS):
                        ahead = max_steps(kind, i, g, n)
                        for half in range(2):
                            for t in tasks_at(kind, g, 2 * n + half):
                                if t[0] == "MT":
                                    split_maxima(kind, i, t, 4 * i + g + 1)
                            if ahead:
                                max_take(*ahead, (2 * half, 2 * half + 1))
                            for t in parts_at("vector", kind, g, 2 * n + half):
                                task(kind, i, g, t)

            def epilogue():
                for t in EPI:
                    task("epi", B, 0, t)

            run(dve, body, prologue, epilogue)

        @block.gpsimd
        def _(pool):
            def mask(i, g, n):
                pool.wait_ge(exp_done, GH * (STEPS * (4 * i + g) + n + 1))
                stand(pool, pool_stand)
                t = pexp[:, GH * (n % 2):GH * (n % 2) + GH, 0:P]
                nc.gpsimd.affine_select(out=t, in_=t, compare_op=ALU.is_ge, fill=0.0, base=0,
                                        pattern=[[0, GH], [1, P]], channel_multiplier=-1).then_inc(tri_done, 1)

            def task(kind, i, g, t):
                if t[0] == "LNA":
                    pool.wait_ge(ln_chain, LN_EACH * (ln_number(kind, i) + 1))
                    stand(pool, pool_stand)
                    normalise(nc.gpsimd, t[1])
                if t[0] == "QK":
                    _, hf, which, c = t
                    pool.wait_ge(qk_second, BY["QK"].at(kind, i, t))
                    part = parts[:, which, :, c * CH:(c + 1) * CH]
                    nc.gpsimd.tensor_tensor(part[:, 2, :], qkr[:, c, :], part[:, 1, :], ALU.subtract)\
                        .then_inc(qk_third, 1)
                if t[0] == "UP":
                    _, c, m = t
                    pool.wait_ge(h_high, BY["UP"].at(kind, i, t))
                    nc.gpsimd.tensor_tensor(hT[:, 1, m, :], gu[:, m % 2, :], hT[:, 0, m, :], ALU.subtract)\
                        .then_inc(h_low, 1)
                if t[0] == "FIN_P":
                    _, tp = t
                    wait_done(pool, kind, i, t)
                    s = so[:, tp % 2, :]
                    nc.gpsimd.tensor_tensor(s, s, g2[:, 2 * tp:2 * tp + 2, :].rearrange("p t c -> p (t c)"),
                                            ALU.mult).then_inc(so_scaled, 1)

            def set_ones(groups):
                return pool.memset(k_st[MROW:MROW + 3, groups, :, :].rearrange("p g j n -> p (g j n)").bitcast(fp32),
                                   float(np.uint32(0x3F803F80).view(np.float32)))

            def prologue():
                pool.memset(ident[:, :], 0.0).then_inc(const0, 1)
                pool.memset(ident16[:, :], 0.0).then_inc(const0, 1)
                pool.memset(tri[:, :], 0.0).then_inc(const0, 1)
                pool.wait_ge(const0, 3)
                for m in (ident, ident16):
                    pool.affine_select(out=m[:, :], in_=m[:, :], compare_op=ALU.not_equal, fill=1.0, base=0,
                                       pattern=[[-1, P]], channel_multiplier=1).then_inc(const_ready, 1)
                pool.wait_ge(const_ready, 2)
                set_ones(slice(0, 2)).then_inc(const_ready, 1)
                pool.wait_ge(const_ready, 3)
                pool.affine_select(out=tri[:, CH - P:CH], in_=tri[:, CH - P:CH], compare_op=ALU.is_ge, fill=NEG,
                                   base=0, pattern=[[-1, P]], channel_multiplier=1).then_inc(const_ready, 1)
                pool.wait_ge(const_ready, 4)
                pool.wait_ge(w_in["rope"], 32)
                pool.wait_ge(w_in["bias"], 16)
                bv = b_row[:, :].rearrange("p (n two) -> p n two", two=2)
                turn(pool, bv[:, :, 0], bv[:, :, 1], g2[0:1, 0, :], g2[0:1, 1, :],
                     [pexp[0:1, 4 + k, 0:C] for k in range(4)], b_chain).then_inc(b_turned, 1)
                pool.wait_ge(w_in["attn"], 16)
                wv = w_qkv[:, :, 0:2 * C].rearrange("p k (n two) -> p k n two", two=2)
                cos, sin = (g2[:, k:k + 1, :] for k in range(2))
                tmp = [pexp[:, k, :].rearrange("p (k n) -> p k n", k=2) for k in range(4)]
                turn(pool, wv[:, :, :, 0], wv[:, :, :, 1], cos.broadcast_to([P, 2, C]), sin.broadcast_to([P, 2, C]),
                     tmp, w_chain).then_inc(w_ready, 1)
                pool.wait_ge(w_ready, 1)
                pool.memset(v_pad[:, :, 0:8, D:D + 1], 1.0).then_inc(ones_ready, 1)
                pool.memset(v_pad[:, :, 8:16, D:D + 1], 1.0).then_inc(ones_ready, 1)
                for t in parts_of("gpsimd", PRO):
                    if t[0] != "LNA":
                        task("pro", 0, 0, t)
                pool.wait_ge(qk_third, 4)
                set_ones(slice(2, 4)).then_inc(const_ready, 1)
                pool.wait_ge(const_ready, 5)
                for name, w in (("gate", w_ga), ("up", w_up), ("down", w_dn)):
                    pool.wait_ge(w_in[name], 16)
                    nc.gpsimd.tensor_copy(w[:, :, :], w_raw[name]).then_inc(w_ready, 1)

            def body(kind, i):
                for g in range(GROUPS):
                    for n in range(STEPS):
                        for half in range(2):
                            for t in parts_at("gpsimd", kind, g, 2 * n + half):
                                task(kind, i, g, t)
                        if is_diag(n):
                            mask(i, g, n)

            def epilogue():
                for t in parts_of("gpsimd", EPI):
                    task("epi", B, 0, t)

            run(pool, body, prologue, epilogue)


_OUT = ((B, T, C), "float32")


def kernel(**inputs):
    import concourse.bacc as _bacc
    from concourse import mybir as _mybir
    from concourse.bass_utils import run_bass_kernel_spmd as _run

    theta = 1.0 / np.power(np.float32(10000.0), np.arange(0, D, 2, dtype=np.float32) / np.float32(D))
    angle = (np.arange(H, dtype=np.float32)[:, None] * theta.astype(np.float32)[None, :]).astype(np.float32)
    tables = {n: np.ascontiguousarray(np.broadcast_to(np.tile(f(angle).astype(np.float32).reshape(1, -1), (1, 2)),
                                                      (P, C)))
              for n, f in (("rope_cos", np.cos), ("rope_sin", np.sin))}
    arrays = {
        "x": np.asarray(inputs["L0_attn_x"]),
        "w_attn": np.asarray(inputs["L0_attn_W_attn"]),
        "b_attn": np.asarray(inputs["L0_attn_b_attn"]).reshape(1, -1),
        "w_proj": np.asarray(inputs["L0_attn_W_proj"]),
        "b_proj": np.asarray(inputs["L0_attn_b_proj"]).reshape(1, -1),
        "w_gate_t": np.asarray(inputs["L0_ffn_w_gate"]).T,
        "w_up_t": np.asarray(inputs["L0_ffn_w_up"]).T,
        "w_down_t": np.asarray(inputs["L0_ffn_w_down"]).T,
        **tables,
    }
    nc = _bacc.Bacc("TRN2", target_bir_lowering=False, num_devices=1)
    maps, args = {}, []
    for name, a in arrays.items():
        a = np.ascontiguousarray(a)
        maps[f"in_{name}"] = a
        args.append(nc.dram_tensor(f"in_{name}", a.shape, _mybir.dt.from_np(a.dtype), kind="ExternalInput").ap())
    shape, dtype = _OUT
    out = nc.dram_tensor("out_0", shape, _mybir.dt.from_np(np.dtype(dtype)), kind="ExternalOutput").ap()
    build_program(nc, *args, out)
    r = _run(nc, [maps], core_ids=[0])
    return r.results[0]["out_0"]
```
